# Optimizing a Trainium2 kernel written in Bass

```python
import numpy as np
import jax
import jax.numpy as jnp

def _softmax(x, axis=-1):
    return jax.nn.softmax(x, axis=axis)

def _gelu(x):
    return jax.nn.gelu(x, approximate=True)

def _silu(x):
    return jax.nn.silu(x)

def _sigmoid(x):
    return jax.nn.sigmoid(x)

def _layernorm(x, axis=-1, eps=1e-05):
    m = jnp.mean(x, axis=axis, keepdims=True)
    v = jnp.var(x, axis=axis, keepdims=True)
    return (x - m) / jnp.sqrt(v + eps)

def _scatter_add(tgt, idx, src, axis=0):
    return tgt.at[idx].add(src)

def _segment_sum(src, seg, n):
    return jax.ops.segment_sum(src, seg, n)
kernel_name = 'mk_macaron_d1_jaxref_r8_0a61a7'

def setup_inputs(seed: int=0):
    np.random.seed(seed)
    _w = jnp.asarray

    def _L0_attn_setup():
        import jax, jax.numpy as jnp
        import numpy as np
        DIM = 128

        def _wkv_scan(k, v, u, w):
            kT = jnp.swapaxes(k, 0, 1)
            vT = jnp.swapaxes(v, 0, 1)

            def step(carry, kv_t):
                a, b = carry
                k_t, v_t = kv_t
                q = jnp.maximum(u + k_t, w)
                e1 = jnp.exp(-w - q)
                e2 = jnp.exp(u + k_t - q)
                a = e1 * a + e2 * v_t
                b = e1 * b + e2
                return ((a, b), a / b)
            B, _, d = k.shape
            init = (jnp.zeros((B, d), k.dtype), jnp.zeros((B, d), k.dtype))
            _, wkvT = jax.lax.scan(step, init, (kT, vT))
            return jnp.swapaxes(wkvT, 0, 1)
        key = jax.random.key(seed)
        ks = jax.random.split(key, 12)
        d = DIM
        B, T = (8, 512)
        s = 1.0 / np.sqrt(d)
        return {'x': jax.random.normal(ks[0], (B, T, d), dtype=jnp.float32), 'u': jnp.ones((d,), dtype=jnp.float32), 'w': jnp.ones((d,), dtype=jnp.float32), 'tmk': jnp.ones((d,), dtype=jnp.float32), 'tmv': jnp.ones((d,), dtype=jnp.float32), 'tmr': jnp.ones((d,), dtype=jnp.float32), 'Wk': jax.random.normal(ks[1], (d, d), dtype=jnp.float32) * s, 'Wv': jax.random.normal(ks[2], (d, d), dtype=jnp.float32) * s, 'Wr': jax.random.normal(ks[3], (d, d), dtype=jnp.float32) * s, 'Wo': jax.random.normal(ks[4], (d, d), dtype=jnp.float32) * s, 'bo': jnp.zeros((d,), dtype=jnp.float32)}
    _L0_attn_in = _L0_attn_setup()

    def _L0_ffn_setup():
        import jax, jax.numpy as jnp
        import numpy as np
        D_MODEL = 128
        EXPERT_DIM = 128
        NUM_EXPERTS = 8
        TOP_K = 2
        B, T = (8, 512)
        key = jax.random.key(seed)
        ks = jax.random.split(key, 5)
        scale_in = 1.0 / np.sqrt(D_MODEL)
        scale_h = 1.0 / np.sqrt(EXPERT_DIM)
        return {'x': jax.random.normal(ks[0], (B, T, D_MODEL), dtype=jnp.float32), 'gate_w': jax.random.normal(ks[1], (D_MODEL, NUM_EXPERTS), dtype=jnp.float32) * scale_in, 'gate_b': jnp.zeros((NUM_EXPERTS,), dtype=jnp.float32), 'w1': jax.random.normal(ks[2], (NUM_EXPERTS, D_MODEL, EXPERT_DIM), dtype=jnp.float32) * scale_in, 'b1': jnp.zeros((NUM_EXPERTS, EXPERT_DIM), dtype=jnp.float32), 'w2': jax.random.normal(ks[3], (NUM_EXPERTS, EXPERT_DIM, D_MODEL), dtype=jnp.float32) * scale_h, 'b2': jnp.zeros((NUM_EXPERTS, D_MODEL), dtype=jnp.float32)}
    _L0_ffn_in = _L0_ffn_setup()
    _d = {'L0_attn_x': _L0_attn_in['x'], 'L0_attn_u': _L0_attn_in['u'], 'L0_attn_w': _L0_attn_in['w'], 'L0_attn_tmk': _L0_attn_in['tmk'], 'L0_attn_tmv': _L0_attn_in['tmv'], 'L0_attn_tmr': _L0_attn_in['tmr'], 'L0_attn_Wk': _L0_attn_in['Wk'], 'L0_attn_Wv': _L0_attn_in['Wv'], 'L0_attn_Wr': _L0_attn_in['Wr'], 'L0_attn_Wo': _L0_attn_in['Wo'], 'L0_attn_bo': _L0_attn_in['bo'], 'L0_ffn_gate_w': _L0_ffn_in['gate_w'], 'L0_ffn_gate_b': _L0_ffn_in['gate_b'], 'L0_ffn_w1': _L0_ffn_in['w1'], 'L0_ffn_b1': _L0_ffn_in['b1'], 'L0_ffn_w2': _L0_ffn_in['w2'], 'L0_ffn_b2': _L0_ffn_in['b2']}
    _x0 = _d['L0_attn_x']
    _d['L0_attn_x'] = jax.random.normal(jax.random.fold_in(jax.random.key(seed), 1), (8, 1024, 128), dtype=_x0.dtype)
    del _x0
    return _d

def reference(L0_attn_x, L0_attn_u, L0_attn_w, L0_attn_tmk, L0_attn_tmv, L0_attn_tmr, L0_attn_Wk, L0_attn_Wv, L0_attn_Wr, L0_attn_Wo, L0_attn_bo, L0_ffn_gate_w, L0_ffn_gate_b, L0_ffn_w1, L0_ffn_b1, L0_ffn_w2, L0_ffn_b2):

    def _L0_attn_ref(x, u, w, tmk, tmv, tmr, Wk, Wv, Wr, Wo, bo):
        import jax, jax.numpy as jnp
        import numpy as np
        DIM = 128

        def _wkv_scan(k, v, u, w):
            kT = jnp.swapaxes(k, 0, 1)
            vT = jnp.swapaxes(v, 0, 1)

            def step(carry, kv_t):
                a, b = carry
                k_t, v_t = kv_t
                q = jnp.maximum(u + k_t, w)
                e1 = jnp.exp(-w - q)
                e2 = jnp.exp(u + k_t - q)
                a = e1 * a + e2 * v_t
                b = e1 * b + e2
                return ((a, b), a / b)
            B, _, d = k.shape
            init = (jnp.zeros((B, d), k.dtype), jnp.zeros((B, d), k.dtype))
            _, wkvT = jax.lax.scan(step, init, (kT, vT))
            return jnp.swapaxes(wkvT, 0, 1)
        x_sh = jnp.pad(x, ((0, 0), (1, 0), (0, 0)))[:, :-1, :]
        key = x * tmk + x_sh * (1.0 - tmk)
        value = x * tmv + x_sh * (1.0 - tmv)
        receptance = jax.nn.sigmoid(x * tmr + x_sh * (1.0 - tmr))
        k = jnp.einsum('btd,ed->bte', key, Wk)
        v = jnp.einsum('btd,ed->bte', value, Wv)
        r = jnp.einsum('btd,ed->bte', receptance, Wr)
        wkv = _wkv_scan(k, v, u, w)
        return jnp.einsum('btd,ed->bte', wkv * r, Wo) + bo

    def _L0_ffn_ref(x, gate_w, gate_b, w1, b1, w2, b2):
        import jax, jax.numpy as jnp
        import numpy as np
        D_MODEL = 128
        EXPERT_DIM = 128
        NUM_EXPERTS = 8
        TOP_K = 2
        B, T = (8, 512)
        b, t, d = x.shape
        xf = x.reshape(b * t, d)
        scores = xf @ gate_w + gate_b
        topk_s, topk_i = jax.lax.top_k(scores, TOP_K)
        n = xf.shape[0]
        comb = jnp.zeros_like(scores).at[jnp.arange(n)[:, None], topk_i].add(topk_s)
        h = jnp.maximum(jnp.einsum('nd,edh->neh', xf, w1) + b1, 0.0)
        eo = jnp.einsum('neh,ehd->ned', h, w2) + b2
        out = jnp.einsum('ne,ned->nd', comb, eo)
        return out.reshape(b, t, d)
    x = L0_attn_x
    x = x + 0.5 * _L0_ffn_ref(_layernorm(x, axis=-1), L0_ffn_gate_w, L0_ffn_gate_b, L0_ffn_w1, L0_ffn_b1, L0_ffn_w2, L0_ffn_b2)
    x = x + _L0_attn_ref(_layernorm(x, axis=-1), L0_attn_u, L0_attn_w, L0_attn_tmk, L0_attn_tmv, L0_attn_tmr, L0_attn_Wk, L0_attn_Wv, L0_attn_Wr, L0_attn_Wo, L0_attn_bo)
    x = x + 0.5 * _L0_ffn_ref(_layernorm(x, axis=-1), L0_ffn_gate_w, L0_ffn_gate_b, L0_ffn_w1, L0_ffn_b1, L0_ffn_w2, L0_ffn_b2)
    return x

_drawn_inputs = setup_inputs


def setup_inputs(seed=0):
    import zlib

    import numpy as np

    out = dict(_drawn_inputs(seed))
    spreads = {'L0_attn_u': (1.0, 0.2),
     'L0_attn_w': (1.0, 0.2),
     'L0_attn_tmk': (1.0, 0.2),
     'L0_attn_tmv': (1.0, 0.2),
     'L0_attn_tmr': (1.0, 0.2),
     'L0_attn_bo': (0.0, 0.1),
     'L0_ffn_gate_b': (0.0, 0.1),
     'L0_ffn_b1': (0.0, 0.1),
     'L0_ffn_b2': (0.0, 0.1)}
    factors = {}
    for name, (base, spread) in spreads.items():
        noise = np.random.default_rng([zlib.crc32(name.encode()), seed]).standard_normal(out[name].shape)
        drawn = base * np.exp(spread * noise) if base else spread * noise
        out[name] = jnp.asarray(drawn.astype(out[name].dtype))
    for name, factor in factors.items():
        out[name] = (out[name] * factor).astype(out[name].dtype)
    return out
```

```python
from contextlib import ExitStack

import concourse.bass as bass
from concourse import mybir

P = 128
F32 = mybir.dt.float32
F32R = mybir.dt.float32r
ALU = mybir.AluOpType
ACT = mybir.ActivationFunctionType
AX = mybir.AxisListType

UNIT = 512
TILES = UNIT // P
LN_EPS = 1e-5
Z_BANKS = 3
G_RING = 4
BC_RING = 8
BC_AHEAD = 2
Z_AHEAD = 2

SLOT = [
    "F", ("ffn1_lo", -2), ("mix", -1),
    "F", ("res1_T", -3), ("kv", -1),
    "F", ("res1", -3), ("ffn1_score", -2), ("ffn0_stat", 1),
    "F", ("ev", -1), ("ffn1_scoreT", -2), ("ffn0_norm", 1),
    "F", ("ffn1_gate", -2), ("r", -1),
    "F", ("rcp0", -1), ("ffn0_yT", 1), ("ffn1_combT", -2),
    "F", ("rcp1", -1), ("ffn1_head", -2),
    "F", ("rcp2", -1), ("ffn0_lo", 1),
    "F", ("rcp3", -1), ("ffn0_score", 1),
    "F", ("wkv", -1), ("res0_T", 0),
    "F", ("res0", 0), ("ln_stat", 0), ("o", -1), ("ffn0_scoreT", 1),
    "F", ("ln_norm", 0), ("ffn0_gate", 1), ("oT", -1),
    "F", ("x2", -1), ("ffn1_stat", -1),
    "F", ("y2T", 0), ("ffn1_norm", -1), ("ffn0_combT", 1),
    "F", ("ffn0_head", 1),
    "F", ("ffn1_yT", -1),
]
TAIL = [
    [("ffn1_lo", -2), ("mix", -1), ("res1_T", -3), ("kv", -1), ("res1", -3), ("ffn1_score", -2), ("ffn1_scoreT", -2),
     ("ffn1_gate", -2), ("ffn1_combT", -2), ("ev", -1), ("r", -1), ("ffn1_head", -2),
     "F", ("rcp0", -1), ("rcp1", -1), "F", ("rcp2", -1), ("rcp3", -1), "F", ("wkv", -1), "F", ("o", -1), "F",
     ("oT", -1), ("x2", -1), ("ffn1_stat", -1), "F", ("ffn1_norm", -1), ("ffn1_yT", -1), "F", "F"],
    [("ffn1_lo", -2), ("res1_T", -3), ("ffn1_score", -2), ("res1", -3), ("ffn1_scoreT", -2), ("ffn1_gate", -2), ("ffn1_combT", -2),
     ("ffn1_head", -2)] + ["F"] * 8,
    [("res1_T", -3), ("res1", -3)],
]
TR_USES = [("res1_T", -3), ("ffn0_yT", 1), ("res0_T", 0), ("oT", -1), ("y2T", 0), ("ffn1_yT", -1)]
SM_USES = [("ffn1_score", -2), ("ffn1_scoreT", -2), ("ffn1_combT", -2),
           ("ffn0_score", 1), ("ffn0_scoreT", 1), ("ffn0_combT", 1)]
GATE_STEPS = 13
HEAD_TURNS = 3
WRITTEN = 3


class Turn:

    def __init__(self, it=None):
        self.it = it

    def v(self, first, per):
        return first if self.it is None else self.it * per + (first - WRITTEN * per)


def macaron_kernel(nc, x, u, w, tmk, tmv, tmr, wk, wv, wr, wo, bo, gate_w, gate_b, w1, b1, w2, b2, out):
    B, T, D = x.shape
    E = w1.shape[0]
    UNITS = B * T // UNIT
    SLOTS = UNITS + 3
    assert D == P and w1.shape[2] == P and T == 2 * UNIT and UNITS % 2 == 0

    def exists(unit):
        return 0 <= unit < UNITS

    BLOCKS = [(f, s - 2 * f, e) for s in range(SLOTS) for f in range(2) if exists(s - 2 * f) for e in range(E)]
    FIRST = {(f, n): i for i, (f, n, e) in reversed(list(enumerate(BLOCKS))) if e == 0}
    PER = 4 * E
    HEAD = 2 * E

    def z_bank(n):
        return (n + 1) % Z_BANKS if n < HEAD else (n - HEAD) % PER % Z_BANKS

    def z_before(n):
        return next((k for k in range(n - 1, -1, -1) if z_bank(k) == z_bank(n)), None)

    def uses(table, step, slot):
        at = [name for name, _ in table].index(step)
        return (sum(exists(s + off) for s in range(-1, slot) for _, off in table)
                + sum(exists(slot + off) for _, off in table[:at]))

    def last_use(table, step, slot):
        at = [name for name, _ in table].index(step)
        past = [(name, t + off) for t in (slot - 1, slot) for name, off in (table if t < slot else table[:at])
                if exists(t + off)]
        return past[-1] if past else None

    x_u = x.rearrange("b (h c p) d -> (b h) p c d", c=TILES, p=P)
    out_u = out.rearrange("b (h c p) d -> (b h) p c d", c=TILES, p=P)

    with ExitStack() as ctx:
        def sb(name, shape, dt=F32):
            return ctx.enter_context(nc.sbuf_tensor(name, shape, dt))

        def sem(name):
            return ctx.enter_context(nc.semaphore(name))

        def bank(name):
            return ctx.enter_context(nc.psum_tensor(name, [P, UNIT], F32))

        ident = sb("ident", [P, P])
        w1_f = sb("w1_f", [P, E, P])
        w1_hi = sb("w1_hi", [P, E, P], F32R)
        w1_lo = sb("w1_lo", [P, E, P], F32R)
        w2_f = sb("w2_f", [P, E, P])
        gate_f = sb("gate_f", [P, E])
        gate_hi = sb("gate_hi", [P, P], F32R)
        gate_lo = sb("gate_lo", [P, P], F32R)
        gate_bias = sb("gate_bias", [E, 1])
        att_w = sb("att_w", [P, 4, P])
        att_wT = sb("att_wT", [P, 4, P])
        NV = 6 + E
        rows = sb("rows", [NV, P])
        cols = sb("cols", [P, NV])
        neg_b1 = sb("neg_b1", [P, E])
        u_minus_w = sb("u_minus_w", [P, 1])
        w_minus_u = sb("w_minus_u", [P, 1])
        neg_2w = sb("neg_2w", [P, 1])
        b1_diag = sb("b1_diag", [P, E, E])
        b2_f = sb("b2_f", [E, P])
        b2_all = sb("b2_all", [E, P])
        prio = sb("prio", [P, TILES, E])
        neg_half = sb("neg_half", [P, TILES])
        col = {name: cols[:, k:k + 1] for k, name in enumerate(["tmk", "tmv", "tmr", "u", "w", "bo"])}

        X0 = sb("X0", [P, 2, TILES, P])
        X1 = sb("X1", [P, 2, TILES, P])
        X2 = sb("X2", [P, 2, TILES, P])
        OUT = sb("OUT", [P, 2, TILES, P])
        LN = ["ffn0", "ln", "ffn1"]
        st = {k: sb(f"st_{k}", [P, TILES, 6]) for k in LN}
        mv = {k: sb(f"mv_{k}", [P, TILES, 2]) for k in LN}
        veps = {k: sb(f"veps_{k}", [P, TILES]) for k in LN}
        nmean = {k: sb(f"nmean_{k}", [P, TILES]) for k in LN}
        rstd = {k: sb(f"rstd_{k}", [P, TILES]) for k in LN}
        shift = {k: sb(f"shift_{k}", [P, TILES]) for k in LN}
        Y = {k: sb(f"Y_{k}", [P, TILES, P]) for k in LN}
        y_hi = [sb(f"y_hi{f}", [P, 2, UNIT], F32R) for f in range(2)]
        y_lo = [sb(f"y_lo{f}", [P, 2, UNIT], F32R) for f in range(2)]
        scT = sb("scT", [E, UNIT])
        sc = sb("sc", [P, TILES, E])
        top = sb("top", [P, TILES])
        hit = sb("hit", [P, TILES, E])
        sel1 = sb("sel1", [P, TILES, E])
        rest = sb("rest", [P, TILES, E])
        sel2 = sb("sel2", [P, TILES, E])
        both = sb("both", [P, TILES, E])
        comb = sb("comb", [P, TILES, E])
        combT = [sb(f"combT{f}", [E, 2, UNIT]) for f in range(2)]
        comb_row = [sb(f"comb_row{f}", [1, 2, E * UNIT]) for f in range(2)]
        BC = sb("BC", [P, BC_RING, UNIT])
        G = sb("G", [P, G_RING, UNIT])
        ffn_oT = [sb(f"ffn_oT{f}", [P, UNIT]) for f in range(2)]
        yT = sb("yT", [P, 1 + T])
        diff = sb("diff", [P, UNIT])
        key_in = sb("key_in", [P, UNIT])
        val_in = sb("val_in", [P, UNIT])
        rec_in = sb("rec_in", [P, UNIT])
        rec_t = sb("rec_t", [P, UNIT])
        rec_s = sb("rec_s", [P, UNIT])
        over = sb("over", [P, UNIT])
        under = sb("under", [P, UNIT])
        e1 = sb("e1", [P, UNIT])
        e2 = sb("e2", [P, UNIT])
        ev = sb("ev", [P, UNIT])
        A_ = sb("A_", [P, T])
        B_ = sb("B_", [P, T])
        rcp = sb("rcp", [P, UNIT])
        wkv = sb("wkv", [P, UNIT])
        wkvr = sb("wkvr", [P, UNIT])
        att_oT = sb("att_oT", [P, UNIT])

        Z = [bank(f"Z{k}") for k in range(Z_BANKS)]
        ACC = bank("ACC")
        TR = bank("TR")
        SM = bank("SM")
        KR = bank("KR")
        VO = bank("VO")

        s_w1 = sem("w1_in")
        s_w2 = sem("w2_in")
        s_small = sem("small_in")
        s_attw = sem("attw_in")
        s_gate = sem("gate_in")
        s_zero = sem("zeroed")
        s_ident = sem("ident_made")
        s_const = sem("const_made")
        s_prio = sem("prio_made")
        s_rowsT = sem("rows_turned")
        s_cols = sem("cols_made")
        s_vec = sem("vectors_made")
        s_w1hi = sem("w1_hi_made")
        s_w1lo = sem("w1_lo_made")
        s_ghi = sem("gate_hi_made")
        s_glo = sem("gate_lo_made")
        s_wT = sem("att_w_turned")
        s_wTs = sem("att_wT_made")
        s_b2m = sem("b1_w2_made")
        s_b2 = sem("b2_all_made")
        x_in = [sem(f"x_in{q}") for q in range(2)]
        stats = {k: sem(f"stats_{k}") for k in LN}
        moments = {k: sem(f"moments_{k}") for k in LN}
        var_eps = {k: sem(f"var_eps_{k}") for k in LN}
        rstd_ok = {k: sem(f"rstd_{k}_ok") for k in LN}
        scaled = {k: sem(f"scale_shift_{k}") for k in LN}
        normed = {k: sem(f"normed_{k}") for k in LN}
        tr_full = sem("tr_full")
        sm_full = sem("sm_full")
        sc_copied = [sem(f"sc_copied{f}") for f in range(2)]
        hi_made = [sem(f"hi_made{f}") for f in range(2)]
        lo_made = [sem(f"lo_made{f}") for f in range(2)]
        scT_made = [sem(f"scT_made{f}") for f in range(2)]
        gate_step = [sem(f"gate_step{f}") for f in range(2)]
        combT_made = [sem(f"combT_made{f}") for f in range(2)]
        row_in = [[sem(f"row_in{f}{q}") for q in range(2)] for f in range(2)]
        bc_made = sem("bc_made")
        z_full = sem("z_full")
        g_made = sem("g_made")
        g_used = sem("g_used")
        acc_read = sem("acc_read")
        x1_made = sem("x1_made")
        x2_made = sem("x2_made")
        out_made = sem("out_made")
        out_done = [sem(f"out_done{q}") for q in range(2)]
        yT_made = sem("yT_made")
        diff_made = sem("diff_made")
        mixed = sem("mixed")
        tanh_made = sem("tanh_made")
        rec_made = sem("rec_made")
        k_full = sem("k_full")
        v_full = sem("v_full")
        r_full = sem("r_full")
        o_full = sem("o_full")
        over_made = sem("over_made")
        under_made = sem("under_made")
        e1_made = sem("e1_made")
        e2_made = sem("e2_made")
        ev_made = sem("ev_made")
        a_made = sem("a_made")
        b_made = sem("b_made")
        rcp_made = sem("rcp_made")
        wkv_made = sem("wkv_made")
        wkvr_made = sem("wkvr_made")
        o_read = sem("o_read")

        read_by = {"res1_T": out_made, "ffn0_yT": lo_made[0], "res0_T": x1_made, "oT": x2_made, "y2T": yT_made,
                   "ffn1_yT": lo_made[1], "ffn0_score": scT_made[0], "ffn1_score": scT_made[1],
                   "ffn0_scoreT": sc_copied[0], "ffn1_scoreT": sc_copied[1],
                   "ffn0_combT": combT_made[0], "ffn1_combT": combT_made[1]}

        def apart(eng):
            eng.sem_inc(waited, 1)

        waited = sem("waited")
        block = ctx.enter_context(nc.Block())

        def walk(steps, s, on_block):
            here = [n for n, (f, unit, e) in enumerate(BLOCKS) if unit + 2 * f == s]
            order = SLOT if exists(s) or s < 0 else TAIL[s - UNITS]
            blocks = iter(here)
            for item in order:
                if item == "F":
                    n = next(blocks, None)
                    if n is not None:
                        on_block(n)
                    continue
                step, off = item
                if exists(s + off) and step in steps:
                    steps[step](s, s + off)

        def pipeline(eng, before, one_slot):
            before()
            one_slot(Turn(), -1)
            for s in range(2 * HEAD_TURNS):
                one_slot(Turn(), s)
            with eng.Fori(HEAD_TURNS, UNITS // 2 - 1) as it:
                for s in (2 * WRITTEN, 2 * WRITTEN + 1):
                    one_slot(Turn(it), s)
            for s in range(UNITS - 2, SLOTS):
                one_slot(Turn(), s)

        @block.sync
        def _(sp):
            def load_x(t, q, unit):
                if unit >= 2:
                    sp.wait_ge(x1_made, t.v(unit - 1, 2))
                src = x_u[t.v(unit, 2)] if t.it is not None else x_u[unit]
                sp.dma_start(X0[:, q], src).then_inc(x_in[q], 16)

            def one_slot(t, s):
                def ffn_row(f):
                    def step(s, unit):
                        q = unit % 2
                        sp.wait_ge(combT_made[f], t.v(unit + 1, 2))
                        apart(sp)
                        if unit >= 2:
                            sp.wait_ge(bc_made, t.v(FIRST[f, unit - 2] + E, PER))
                        sp.dma_start(comb_row[f][0:1, q].rearrange("p (e n) -> p e n", e=E),
                                     combT[f][:, q]).then_inc(row_in[f][q], 16)
                    return step

                def load(s, unit):
                    if exists(unit + 2):
                        load_x(t, unit % 2, unit + 2)

                def store(s, unit):
                    q = unit % 2
                    sp.wait_ge(out_made, t.v(unit + 1, 2))
                    dst = out_u[t.v(unit, 2)] if t.it is not None else out_u[unit]
                    sp.dma_start(dst, OUT[:, q]).then_inc(out_done[q], 16)

                walk({"res0": load, "res1": store, "ffn0_combT": ffn_row(0), "ffn1_combT": ffn_row(1)},
                     s, lambda n: None)

            def before():
                load_x(Turn(), 0, 0)
                sp.dma_start(gate_f[:], gate_w).then_inc(s_gate, 16)
                sp.dma_start(gate_bias[:], gate_b.rearrange("(e a) -> e a", a=1)).then_inc(s_gate, 16)
                load_x(Turn(), 1, 1)
                sp.dma_start(att_w[:, 0], wk).then_inc(s_attw, 16)
                sp.dma_start(att_w[:, 1], wv).then_inc(s_attw, 16)
                sp.dma_start(att_w[:, 2], wr).then_inc(s_attw, 16)
                sp.dma_start(att_w[:, 3], wo).then_inc(s_attw, 16)

            pipeline(sp, before, one_slot)
            for q in range(2):
                sp.wait_ge(out_done[q], 16 * UNITS // 2)

        @block.gpsimd
        def _(pool):
            def before():
                nc.gpsimd.memset(ident[:], 0.0).then_inc(s_zero, 1)
                pool.wait_ge(s_zero, 1)
                nc.gpsimd.affine_select(out=ident[:], in_=ident[:], compare_op=ALU.not_equal, fill=1.0, base=0,
                                        pattern=[[-1, P]], channel_multiplier=1).then_inc(s_ident, 1)
                nc.gpsimd.memset(neg_half[:], -0.5).then_inc(s_const, 1)
                pool.wait_ge(s_const, 1)

            def broadcast(t, n):
                f, unit, e = BLOCKS[n]
                if e == 0:
                    pool.wait_ge(row_in[f][unit % 2], t.v(16 * (unit // 2 + 1), 16))
                if n >= BC_RING:
                    pool.wait_ge(g_made, t.v(n - BC_RING + 1, PER))
                apart(pool)
                nc.gpsimd.partition_broadcast(
                    BC[:, n % BC_RING], comb_row[f][0:1, unit % 2, e * UNIT:(e + 1) * UNIT]).then_inc(bc_made, 1)

            def one_slot(t, s):
                def rstd_of(k):
                    def step(s, unit):
                        pool.wait_ge(moments[k], t.v(unit + 1, 2))
                        if unit >= 1:
                            pool.wait_ge(normed[k], t.v(unit, 2))
                        apart(pool)
                        nc.gpsimd.tensor_scalar(veps[k][:], mv[k][:, :, 1], LN_EPS, None, ALU.add).then_inc(var_eps[k], 1)
                        nc.gpsimd.tensor_scalar(nmean[k][:], mv[k][:, :, 0], -1.0, None, ALU.mult).then_inc(var_eps[k], 1)
                        pool.wait_ge(var_eps[k], t.v(2 * (unit + 1), 4))
                        nc.gpsimd.tensor_tensor(rstd[k][:], veps[k][:], neg_half[:], ALU.pow).then_inc(rstd_ok[k], 1)
                        pool.wait_ge(rstd_ok[k], t.v(unit + 1, 2))
                        nc.gpsimd.tensor_tensor(shift[k][:], nmean[k][:], rstd[k][:], ALU.mult).then_inc(scaled[k], 1)
                    return step

                def difference(s, unit):
                    lo = (unit % 2) * UNIT
                    pool.wait_ge(yT_made, t.v(unit + 1, 2))
                    if unit >= 1:
                        pool.wait_ge(mixed, t.v(3 * unit, 6))
                    nc.gpsimd.tensor_tensor(diff[:], yT[:, lo + 1:lo + 1 + UNIT], yT[:, lo:lo + UNIT],
                                            ALU.subtract).then_inc(diff_made, 1)

                def receptance(s, unit):
                    pool.wait_ge(tanh_made, t.v(unit + 1, 2))
                    if unit >= 1:
                        pool.wait_ge(r_full, t.v(unit, 2))
                    apart(pool)
                    nc.gpsimd.tensor_scalar(rec_s[:], rec_t[:], 0.5, 0.5, ALU.mult, ALU.add).then_inc(rec_made, 1)

                def head(f):
                    def step(s, unit):
                        for e in range(BC_AHEAD):
                            broadcast(t, FIRST[f, unit] + e)
                    return step

                def on_block(n):
                    if BLOCKS[n][2] + BC_AHEAD < E:
                        broadcast(t, n + BC_AHEAD)

                walk({"ffn0_stat": rstd_of("ffn0"), "ln_stat": rstd_of("ln"), "ffn1_stat": rstd_of("ffn1"),
                      "y2T": difference, "kv": receptance, "ffn0_head": head(0), "ffn1_head": head(1)}, s, on_block)

            pipeline(pool, before, one_slot)

        @block.scalar
        def _(act):
            def before():
                for k, v in enumerate([tmk, tmv, tmr, u, w, bo]):
                    act.dma_start(rows[k:k + 1, :], v.rearrange("(a d) -> a d", a=1)).then_inc(s_small, 16)
                act.dma_start(rows[6:6 + E, :], b1).then_inc(s_small, 16)
                act.dma_start(b2_f[:], b2).then_inc(s_small, 16)
                act.dma_start(w1_f[:], w1.rearrange("e d h -> d e h")).then_inc(s_w1, 16)
                act.dma_start(w2_f[:], w2.rearrange("e h d -> h e d")).then_inc(s_w2, 16)

            def one_slot(t, s):
                def norm(k, X):
                    def step(s, unit):
                        act.wait_ge(scaled[k], t.v(unit + 1, 2))
                        if unit >= 1:
                            yT_step, off = {"ffn0": ("ffn0_yT", 1), "ln": ("y2T", 0), "ffn1": ("ffn1_yT", -1)}[k]
                            act.wait_ge(tr_full, t.v(uses(TR_USES, yT_step, unit - 1 - off) + 1, 12))
                        for c in range(TILES):
                            last = nc.scalar.activation(Y[k][:, c], X[:, unit % 2, c], ACT.Identity,
                                                        bias=shift[k][:, c:c + 1], scale=rstd[k][:, c:c + 1])
                        last.then_inc(normed[k], 1)
                    return step

                def y_high(f):
                    def step(s, unit):
                        act.wait_ge(tr_full, t.v(uses(TR_USES, f"ffn{f}_yT", s) + 1, 12))
                        if unit >= 2:
                            act.wait_ge(z_full, t.v(FIRST[f, unit - 2] + E, PER))
                            act.wait_ge(sm_full, t.v(uses(SM_USES, f"ffn{f}_score", (unit - 2) + (2 if f else -1)) + 1, 12))
                        nc.scalar.activation(y_hi[f][:, unit % 2], TR[:], ACT.Copy).then_inc(hi_made[f], 1)
                    return step

                def score(f):
                    def step(s, unit):
                        n = uses(SM_USES, f"ffn{f}_score", s)
                        act.wait_ge(sm_full, t.v(n + 1, 12))
                        nc.scalar.activation(scT[:], SM[0:E], ACT.Identity, bias=gate_bias[:, 0:1]).then_inc(scT_made[f], 1)
                    return step

                def comb_turned(f):
                    def step(s, unit):
                        act.wait_ge(sm_full, t.v(uses(SM_USES, f"ffn{f}_combT", s) + 1, 12))
                        if unit >= 2:
                            act.wait_ge(row_in[f][unit % 2], t.v(16 * (unit // 2), 16))
                            act.wait_ge(g_used, t.v(FIRST[f, unit - 2] + 1, PER))
                        nc.scalar.activation(combT[f][:, unit % 2], SM[0:E], ACT.Copy).then_inc(combT_made[f], 1)
                    return step

                def y2_turned(s, unit):
                    lo = (unit % 2) * UNIT
                    act.wait_ge(tr_full, t.v(uses(TR_USES, "y2T", s) + 1, 12))
                    if unit >= 1:
                        act.wait_ge(mixed, t.v(3 * unit, 6))
                    nc.scalar.activation(yT[:, lo + 1:lo + 1 + UNIT], TR[:], ACT.Copy).then_inc(yT_made, 1)

                def tanh(s, unit):
                    act.wait_ge(mixed, t.v(3 * unit + 1, 6))
                    if unit >= 1:
                        act.wait_ge(rec_made, t.v(unit, 2))
                    nc.scalar.activation(rec_t[:], rec_in[:], ACT.Tanh, scale=0.5).then_inc(tanh_made, 1)

                def decays(s, unit):
                    act.wait_ge(k_full, t.v(unit + 1, 2))
                    nc.scalar.activation(over[:], KR[:], ACT.Relu, bias=u_minus_w[:, 0:1]).then_inc(over_made, 1)
                    nc.scalar.activation(under[:], KR[:], ACT.Relu, bias=w_minus_u[:, 0:1], scale=-1.0).then_inc(under_made, 1)
                    act.wait_ge(over_made, t.v(unit + 1, 2))
                    if unit >= 1:
                        act.wait_ge(b_made, t.v(unit, 2))
                    nc.scalar.activation(e1[:], over[:], ACT.Exp, bias=neg_2w[:, 0:1], scale=-1.0).then_inc(e1_made, 1)
                    act.wait_ge(under_made, t.v(unit + 1, 2))
                    nc.scalar.activation(e2[:], under[:], ACT.Exp, scale=-1.0).then_inc(e2_made, 1)

                def att_out(s, unit):
                    act.wait_ge(o_full, t.v(unit + 1, 2))
                    if unit >= 1:
                        act.wait_ge(tr_full, t.v(uses(TR_USES, "oT", s - 1) + 1, 12))
                    nc.scalar.activation(att_oT[:], VO[:], ACT.Identity, bias=col["bo"]).then_inc(o_read, 1)

                def on_block(n):
                    f, unit, e = BLOCKS[n]
                    if e != E - 1:
                        return
                    act.wait_ge(g_used, t.v(n + 1, PER))
                    if unit >= 1:
                        off = (0, -3)[f]
                        act.wait_ge(tr_full, t.v(uses(TR_USES, f"res{f}_T", unit - 1 - off) + 1, 12))
                    nc.scalar.activation(ffn_oT[f][:], ACC[:], ACT.Copy, scale=0.5).then_inc(acc_read, 1)

                if s == -1:
                    act.wait_ge(s_gate, 32)
                if s == 0:
                    act.wait_ge(s_vec, 4)
                walk({"ffn0_norm": norm("ffn0", X0), "ln_norm": norm("ln", X1), "ffn1_norm": norm("ffn1", X2),
                      "ffn0_yT": y_high(0), "ffn1_yT": y_high(1), "ffn0_score": score(0), "ffn1_score": score(1),
                      "ffn0_combT": comb_turned(0), "ffn1_combT": comb_turned(1), "y2T": y2_turned,
                      "mix": tanh, "kv": decays, "o": att_out}, s, on_block)

            pipeline(act, before, one_slot)

        @block.vector
        def _(dve):
            def before():
                nc.vector.memset(yT[:, 0:1], 0.0)
                nc.vector.memset(b1_diag[:], 0.0)
                for e in range(E):
                    nc.vector.memset(prio[:, :, e:e + 1], float(E - e))
                nc.vector.memset(gate_hi[:].bitcast(F32), 0.0)
                nc.vector.memset(gate_lo[:].bitcast(F32), 0.0).then_inc(s_prio, 1)
                dve.wait_ge(s_prio, 1)
                dve.wait_ge(s_gate, 32)
                nc.vector.tensor_copy(gate_hi[:, 0:E], gate_f[:]).then_inc(s_ghi, 1)
                dve.wait_ge(s_ghi, 1)
                nc.vector.tensor_tensor(gate_lo[:, 0:E], gate_f[:], gate_hi[:, 0:E].bitcast(F32),
                                        ALU.subtract).then_inc(s_glo, 1)

            def setup():
                dve.wait_ge(s_w1, 16)
                nc.vector.tensor_copy(w1_hi[:], w1_f[:]).then_inc(s_w1hi, 1)
                dve.wait_ge(s_w1hi, 1)
                nc.vector.tensor_tensor(w1_lo[:], w1_f[:], w1_hi[:].bitcast(F32), ALU.subtract).then_inc(s_w1lo, 1)
                dve.wait_ge(s_rowsT, 1)
                nc.vector.tensor_copy(cols[:], KR[:, 0:NV]).then_inc(s_cols, 1)
                dve.wait_ge(s_cols, 1)
                nc.vector.tensor_scalar(neg_b1[:], cols[:, 6:NV], -1.0, None, ALU.mult).then_inc(s_vec, 1)
                nc.vector.tensor_tensor(u_minus_w[:], col["u"], col["w"], ALU.subtract).then_inc(s_vec, 1)
                nc.vector.tensor_tensor(w_minus_u[:], col["w"], col["u"], ALU.subtract).then_inc(s_vec, 1)
                nc.vector.tensor_scalar(neg_2w[:], col["w"], -2.0, None, ALU.mult).then_inc(s_vec, 1)
                for e in range(E):
                    last = nc.vector.tensor_copy(b1_diag[:, e, e:e + 1], cols[:, 6 + e:7 + e])
                last.then_inc(s_cols, 1)
                dve.wait_ge(s_b2m, 1)
                dve.wait_ge(s_small, 16 * 8)
                nc.vector.tensor_tensor(b2_all[:], VO[0:E, 0:P], b2_f[:], ALU.add).then_inc(s_b2, 1)
                dve.wait_ge(s_wT, 1)
                nc.vector.tensor_copy(att_wT[:].rearrange("p a b -> p (a b)"), KR[:]).then_inc(s_wTs, 1)
                dve.wait_ge(s_vec, 4)

            def one_slot(t, s):
                def stat(k, X):
                    def step(s, unit):
                        if k == "ffn0":
                            dve.wait_ge(x_in[unit % 2], t.v(16 * (unit // 2 + 1), 16))
                        else:
                            dve.wait_ge({"ln": x1_made, "ffn1": x2_made}[k], t.v(unit + 1, 2))
                        if unit >= 1:
                            dve.wait_ge(scaled[k], t.v(unit, 2))
                        for c in range(TILES):
                            last = nc.vector.bn_stats(st[k][:, c], X[:, unit % 2, c])
                        last.then_inc(stats[k], 1)
                        dve.wait_ge(stats[k], t.v(unit + 1, 2))
                        apart(dve)
                        for c in range(TILES):
                            last = nc.vector.bn_aggr(mv[k][:, c], st[k][:, c])
                        last.then_inc(moments[k], 1)
                    return step

                def y_low(f):
                    def step(s, unit):
                        dve.wait_ge(hi_made[f], t.v(unit + 1, 2))
                        nc.vector.tensor_tensor(y_lo[f][:, unit % 2], TR[:], y_hi[f][:, unit % 2].bitcast(F32),
                                                ALU.subtract).then_inc(lo_made[f], 1)
                    return step

                def gate(f):
                    def step(s, unit):
                        done = [0]

                        def then(ins):
                            done[0] += 1
                            ins.then_inc(gate_step[f], 1)
                            dve.wait_ge(gate_step[f], t.v(GATE_STEPS * unit + done[0], 2 * GATE_STEPS))

                        def wide(a):
                            return a[:].unsqueeze(2).to_broadcast([P, TILES, E])

                        dve.wait_ge(sm_full, t.v(uses(SM_USES, f"ffn{f}_scoreT", s) + 1, 12))
                        nc.vector.tensor_copy(sc[:].rearrange("p c e -> p (c e)"), SM[:, 0:TILES * E]).then_inc(sc_copied[f], 1)
                        dve.wait_ge(sc_copied[f], t.v(unit + 1, 2))
                        then(nc.vector.tensor_reduce(top[:], sc[:], AX.X, ALU.max))
                        then(nc.vector.tensor_tensor(hit[:], sc[:], wide(top), ALU.is_equal))
                        then(nc.vector.tensor_tensor(hit[:], hit[:], prio[:], ALU.mult))
                        then(nc.vector.tensor_reduce(top[:], hit[:], AX.X, ALU.max))
                        then(nc.vector.tensor_tensor(sel1[:], hit[:], wide(top), ALU.is_equal))
                        then(nc.vector.scalar_tensor_tensor(out=rest[:], in0=sel1[:], scalar=-3.0e38, in1=sc[:],
                                                            op0=ALU.mult, op1=ALU.add))
                        then(nc.vector.tensor_reduce(top[:], rest[:], AX.X, ALU.max))
                        then(nc.vector.tensor_tensor(hit[:], rest[:], wide(top), ALU.is_equal))
                        then(nc.vector.tensor_tensor(hit[:], hit[:], prio[:], ALU.mult))
                        then(nc.vector.tensor_reduce(top[:], hit[:], AX.X, ALU.max))
                        then(nc.vector.tensor_tensor(sel2[:], hit[:], wide(top), ALU.is_equal))
                        then(nc.vector.tensor_tensor(both[:], sel1[:], sel2[:], ALU.add))
                        then(nc.vector.tensor_tensor(comb[:], both[:], sc[:], ALU.mult))
                        assert done[0] == GATE_STEPS
                    return step

                def residual(name, src, dst, made):
                    def step(s, unit):
                        q = unit % 2
                        n = uses(TR_USES, name, s)
                        dve.wait_ge(tr_full, t.v(n + 1, 12))
                        if name == "res1_T" and unit >= 2:
                            dve.wait_ge(out_done[q], t.v(16 * (unit // 2), 16))
                        nc.vector.tensor_tensor(dst[:, q].rearrange("p c d -> p (c d)"),
                                                src[:, q].rearrange("p c d -> p (c d)"), TR[:], ALU.add).then_inc(made, 1)
                    return step

                def mix(s, unit):
                    lo = (unit % 2) * UNIT
                    dve.wait_ge(diff_made, t.v(unit + 1, 2))
                    if unit >= 1:
                        dve.wait_ge(v_full, t.v(unit, 2))
                        dve.wait_ge(tanh_made, t.v(unit, 2))
                    for name, dst in (("tmr", rec_in), ("tmk", key_in), ("tmv", val_in)):
                        nc.vector.scalar_tensor_tensor(out=dst[:], in0=diff[:], scalar=col[name], in1=yT[:, lo:lo + UNIT],
                                                       op0=ALU.mult, op1=ALU.add).then_inc(mixed, 1)

                def scans(s, unit):
                    lo = (unit % 2) * UNIT
                    dve.wait_ge(e2_made, t.v(unit + 1, 2))
                    dve.wait_ge(v_full, t.v(unit + 1, 2))
                    nc.vector.tensor_tensor(ev[:], VO[:], e2[:], ALU.mult).then_inc(ev_made, 1)
                    first = unit % 2 == 0
                    if not first:
                        dve.wait_ge(b_made, t.v(unit, 2))
                    nc.vector.tensor_tensor_scan(B_[:, lo:lo + UNIT], e1[:], e2[:], 0.0 if first else B_[:, lo - 1:lo],
                                                 ALU.mult, ALU.add).then_inc(b_made, 1)
                    dve.wait_ge(ev_made, t.v(unit + 1, 2))
                    nc.vector.tensor_tensor_scan(A_[:, lo:lo + UNIT], e1[:], ev[:], 0.0 if first else A_[:, lo - 1:lo],
                                                 ALU.mult, ALU.add).then_inc(a_made, 1)

                def rcp_part(k):
                    def step(s, unit):
                        lo = (unit % 2) * UNIT
                        if k == 0:
                            dve.wait_ge(b_made, t.v(unit + 1, 2))
                        nc.vector.reciprocal(rcp[:, k * P:(k + 1) * P], B_[:, lo + k * P:lo + (k + 1) * P]).then_inc(rcp_made, 1)
                    return step

                def weigh(s, unit):
                    lo = (unit % 2) * UNIT
                    dve.wait_ge(rcp_made, t.v(TILES * (unit + 1), 2 * TILES))
                    dve.wait_ge(a_made, t.v(unit + 1, 2))
                    nc.vector.tensor_tensor(wkv[:], A_[:, lo:lo + UNIT], rcp[:], ALU.mult).then_inc(wkv_made, 1)
                    dve.wait_ge(wkv_made, t.v(unit + 1, 2))
                    dve.wait_ge(r_full, t.v(unit + 1, 2))
                    if unit >= 1:
                        dve.wait_ge(o_full, t.v(unit, 2))
                    nc.vector.tensor_tensor(wkvr[:], KR[:], wkv[:], ALU.mult).then_inc(wkvr_made, 1)

                def on_block(n):
                    f, unit, e = BLOCKS[n]
                    dve.wait_ge(z_full, t.v(n + 1, PER))
                    dve.wait_ge(bc_made, t.v(n + 1, PER))
                    if n >= G_RING:
                        dve.wait_ge(g_used, t.v(n - G_RING + 1, PER))
                    nc.vector.scalar_tensor_tensor(out=G[:, n % G_RING], in0=Z[z_bank(n)][:], scalar=neg_b1[:, e:e + 1],
                                                   in1=BC[:, n % BC_RING], op0=ALU.max, op1=ALU.mult).then_inc(g_made, 1)

                steps = {"ffn0_stat": stat("ffn0", X0), "ln_stat": stat("ln", X1), "ffn1_stat": stat("ffn1", X2),
                         "ffn0_lo": y_low(0), "ffn1_lo": y_low(1), "ffn0_gate": gate(0), "ffn1_gate": gate(1),
                         "res0": residual("res0_T", X0, X1, x1_made), "x2": residual("oT", X1, X2, x2_made),
                         "res1": residual("res1_T", X2, OUT, out_made), "mix": mix, "ev": scans, "wkv": weigh}
                steps |= {f"rcp{k}": rcp_part(k) for k in range(TILES)}
                walk(steps, s, on_block)
                if s == -1:
                    setup()

            pipeline(dve, before, one_slot)

        @block.tensor
        def _(pe):
            def before():
                pe.wait_ge(s_ident, 1)

            def setup():
                pe.wait_ge(s_small, 16 * 8)
                nc.tensor.transpose(KR[:, 0:NV], rows[:], ident[0:NV, 0:NV]).then_inc(s_rowsT, 1)
                pe.wait_ge(s_w2, 16)
                pe.wait_ge(s_cols, 2)
                for e in range(E):
                    last = nc.tensor.matmul(VO[0:E, 0:P], b1_diag[:, e], w2_f[:, e], start=(e == 0), stop=(e == E - 1))
                last.then_inc(s_b2m, 1)
                pe.wait_ge(s_attw, 64)
                for k in range(4):
                    last = nc.tensor.transpose(KR[:, k * P:(k + 1) * P], att_w[:, k], ident[:])
                last.then_inc(s_wT, 1)
                pe.wait_ge(s_w1lo, 1)
                for n in range(Z_AHEAD):
                    up(Turn(), n)
                pe.wait_ge(s_b2, 1)
                pe.wait_ge(s_wTs, 1)

            def up(t, n):
                f, unit, e = BLOCKS[n]
                if e == 0:
                    pe.wait_ge(lo_made[f], t.v(unit + 1, 2))
                if (k := z_before(n)) is not None:
                    pe.wait_ge(g_made, t.v(k + 1, PER))
                z = Z[z_bank(n)][:]
                q = unit % 2
                nc.tensor.matmul(z, w1_hi[:, e], y_hi[f][:, q], start=True, stop=False)
                nc.tensor.matmul(z, w1_hi[:, e], y_lo[f][:, q], start=False, stop=False)
                nc.tensor.matmul(z, w1_lo[:, e], y_hi[f][:, q], start=False, stop=True).then_inc(z_full, 1)

            def down(t, n):
                f, unit, e = BLOCKS[n]
                if e == 0:
                    if n >= E:
                        pe.wait_ge(acc_read, t.v(n // E, 4))
                    pe.wait_ge(combT_made[f], t.v(unit + 1, 2))
                    nc.tensor.matmul(ACC[:], b2_all[:], combT[f][:, unit % 2], start=True, stop=False)
                pe.wait_ge(g_made, t.v(n + 1, PER))
                last = nc.tensor.matmul(ACC[:], w2_f[:, e], G[:, n % G_RING], start=False, stop=(e == E - 1))
                last.then_inc(g_used, 1)

            def one_slot(t, s):
                def bank_read(table, step, s):
                    if (past := last_use(table, step, s)) is not None:
                        pe.wait_ge(read_by[past[0]], t.v(past[1] + 1, 2))

                def turn(step_name, source, wait):
                    def step(s, unit):
                        bank_read(TR_USES, step_name, s)
                        wait(unit)
                        for c in range(TILES):
                            last = nc.tensor.transpose(TR[:, c * P:(c + 1) * P], source(c), ident[:])
                        last.then_inc(tr_full, 1)
                    return step

                def y_turn(name, k):
                    return turn(name, lambda c: Y[k][:, c], lambda unit: pe.wait_ge(normed[k], t.v(unit + 1, 2)))

                def ffn_turn(f):
                    return turn(f"res{f}_T", lambda c: ffn_oT[f][:, c * P:(c + 1) * P],
                                lambda unit: pe.wait_ge(acc_read, t.v(FIRST[f, unit] // E + 1, 4)))

                def score(f):
                    def step(s, unit):
                        bank_read(SM_USES, f"ffn{f}_score", s)
                        pe.wait_ge(lo_made[f], t.v(unit + 1, 2))
                        if unit == 0 and f == 0:
                            pe.wait_ge(s_glo, 1)
                        q = unit % 2
                        nc.tensor.matmul(SM[:], gate_hi[:], y_hi[f][:, q], start=True, stop=False)
                        nc.tensor.matmul(SM[:], gate_hi[:], y_lo[f][:, q], start=False, stop=False)
                        nc.tensor.matmul(SM[:], gate_lo[:], y_hi[f][:, q], start=False, stop=True).then_inc(sm_full, 1)
                    return step

                def scores_back(f):
                    def step(s, unit):
                        bank_read(SM_USES, f"ffn{f}_scoreT", s)
                        apart(pe)
                        for c in range(TILES):
                            last = nc.tensor.transpose(SM[:, c * E:(c + 1) * E], scT[:, c * P:(c + 1) * P], ident[0:E, 0:E])
                        last.then_inc(sm_full, 1)
                    return step

                def comb_turn(f):
                    def step(s, unit):
                        pe.wait_ge(gate_step[f], t.v(GATE_STEPS * (unit + 1), 2 * GATE_STEPS))
                        for c in range(TILES):
                            last = nc.tensor.transpose(SM[0:E, c * P:(c + 1) * P], comb[:, c], ident[:])
                        last.then_inc(sm_full, 1)
                    return step

                def keys_values(s, unit):
                    pe.wait_ge(mixed, t.v(3 * (unit + 1), 6))
                    if unit >= 1:
                        pe.wait_ge(wkvr_made, t.v(unit, 2))
                        pe.wait_ge(o_read, t.v(unit, 2))
                    nc.tensor.matmul(KR[:], att_wT[:, 0], key_in[:], start=True, stop=True).then_inc(k_full, 1)
                    nc.tensor.matmul(VO[:], att_wT[:, 1], val_in[:], start=True, stop=True).then_inc(v_full, 1)

                def receptance(s, unit):
                    pe.wait_ge(under_made, t.v(unit + 1, 2))
                    pe.wait_ge(rec_made, t.v(unit + 1, 2))
                    nc.tensor.matmul(KR[:], att_wT[:, 2], rec_s[:], start=True, stop=True).then_inc(r_full, 1)

                def output(s, unit):
                    pe.wait_ge(ev_made, t.v(unit + 1, 2))
                    pe.wait_ge(wkvr_made, t.v(unit + 1, 2))
                    nc.tensor.matmul(VO[:], att_wT[:, 3], wkvr[:], start=True, stop=True).then_inc(o_full, 1)

                def late(unit, f):
                    return unit + 2 * f >= UNITS

                def head(s, unit):
                    if late(unit, 1):
                        for e in range(Z_AHEAD):
                            up(t, FIRST[1, unit] + e)

                def on_block(n):
                    if n + Z_AHEAD < len(BLOCKS):
                        f, unit, e = BLOCKS[n + Z_AHEAD]
                        if not (late(unit, f) and e < Z_AHEAD):
                            up(t, n + Z_AHEAD)
                    down(t, n)

                walk({"res0_T": ffn_turn(0), "res1_T": ffn_turn(1), "ffn0_yT": y_turn("ffn0_yT", "ffn0"),
                      "y2T": y_turn("y2T", "ln"), "ffn1_yT": y_turn("ffn1_yT", "ffn1"),
                      "oT": turn("oT", lambda c: att_oT[:, c * P:(c + 1) * P], lambda unit: pe.wait_ge(o_read, t.v(unit + 1, 2))),
                      "ffn0_score": score(0), "ffn1_score": score(1), "ffn0_scoreT": scores_back(0),
                      "ffn1_scoreT": scores_back(1), "ffn0_combT": comb_turn(0), "ffn1_combT": comb_turn(1),
                      "kv": keys_values, "r": receptance, "o": output, "ffn1_head": head}, s, on_block)
                if s == -1:
                    setup()

            pipeline(pe, before, one_slot)


_INS = ['L0_attn_x', 'L0_attn_u', 'L0_attn_w', 'L0_attn_tmk', 'L0_attn_tmv', 'L0_attn_tmr', 'L0_attn_Wk', 'L0_attn_Wv',
        'L0_attn_Wr', 'L0_attn_Wo', 'L0_attn_bo', 'L0_ffn_gate_w', 'L0_ffn_gate_b', 'L0_ffn_w1', 'L0_ffn_b1',
        'L0_ffn_w2', 'L0_ffn_b2']


def kernel(**inputs):
    import numpy as np
    import concourse.bacc as bacc
    from concourse.bass_utils import run_bass_kernel_spmd

    nc = bacc.Bacc("TRN2", target_bir_lowering=False, num_devices=1)
    arrays, args = {}, []
    for name in _INS:
        a = np.ascontiguousarray(inputs[name])
        arrays[f"in_{name}"] = a
        args.append(nc.dram_tensor(f"in_{name}", a.shape, mybir.dt.from_np(a.dtype), kind="ExternalInput").ap())
    shape = inputs["L0_attn_x"].shape
    out = nc.dram_tensor("out", shape, F32, kind="ExternalOutput").ap()
    macaron_kernel(nc, *args, out)
    r = run_bass_kernel_spmd(nc, [arrays], core_ids=[0])
    return r.results[0]["out"]
```

```python
from contextlib import ExitStack

import concourse.bass as bass
from concourse import mybir

P = 128
F32 = mybir.dt.float32
F32R = mybir.dt.float32r
I32 = mybir.dt.int32
ALU = mybir.AluOpType
ACT = mybir.ActivationFunctionType
AX = mybir.AxisListType

UNIT = 512
TILES = UNIT // P
LN_EPS = 1e-5
Z_BANKS = 3
G_RING = 4
BC_RING = 8
BC_AHEAD = 4
Z_AHEAD = 3

SLOT = [
    "F", ("res1_T", -3), ("ffn1_score", -2),
    "F", ("scoreT", None), ("ffn0_norm", 2),
    "F", ("mix", -1), ("ffn1_lo", -2), ("kv", -1),
    "F", ("res1", -3), ("sigmoid", -1), ("ffn1_combT", -2),
    "F", ("r", -1), ("ffn1_head", -2), ("gate", None), ("gate2", None),
    "F",
    "F", ("ev", -1),
    "F", ("ffn0_yT", 2), ("rcp0", -1), ("rcp1", -1), ("rcp2", -1),
    "F", ("res0_T", 0),
    "F", ("o", -1), ("ffn0_combT", 1), ("rcp3", -1), ("oT", -1), ("ffn0_stat", 3),
    "F", ("wkv", -1),
    "F", ("res0", 0),
    "F", ("ln_stat", 0), ("x2", -1),
    "F", ("ffn1_stat", -1),
    "F", ("rstd", None), ("ln_norm", 0), ("ffn1_norm", -1), ("y2T", 0),
    "F", ("ffn1_yT", -1), ("ffn0_head", 1), ("ffn0_score", 2), ("ffn0_lo", 2),
]
OPENING = [
    [
        ("ffn0_stat", 3), ("rstd", None),
    ],
    [
        ("w1", None), ("ffn0_stat", 3), ("gate_w", None), ("rstd", None), ("ffn0_norm", 2), ("ffn0_yT", 2),
        ("ffn0_lo", 2), ("ffn0_score", 2),
    ],
    [
        ("rows", None), ("scoreT", None), ("ffn0_stat", 3), ("ffn0_norm", 2), ("vectors", None), ("b2_rows", None),
        ("gate", None), ("att_turn", None), ("ffn0_yT", 2), ("gate2", None), ("b2", None), ("ffn0_lo", 2),
        ("ffn0_combT", 1), ("ffn0_score", 2), ("rstd", None), ("first_z", None), ("ffn0_head", 1),
    ],
    [
        ("ffn0_norm", 2),
        "F", "F", "F",
        "F", ("scoreT", None),
        "F", "F",
        "F", ("gate", None),
        "F", ("ffn0_combT", 1), ("gate2", None), ("att_w", None), ("ffn0_stat", 3), ("res0", 0), ("ln_stat", 0),
        ("rstd", None), ("ffn0_head", 1), ("res0_T", 0), ("ffn0_yT", 2), ("ln_norm", 0), ("ffn0_score", 2),
        ("ffn0_lo", 2), ("y2T", 0),
    ],
    [
        "F",
        "F", ("sigmoid", -1), ("scoreT", None),
        "F",
        "F", ("kv", -1), ("mix", -1),
        "F", ("gate", None), ("gate2", None),
        "F", ("r", -1),
        "F", ("ffn0_norm", 2),
        "F", ("ev", -1), ("rcp0", -1), ("rcp1", -1), ("res0_T", 0), ("rcp2", -1), ("rcp3", -1), ("ffn0_combT", 1),
        ("wkv", -1), ("res0", 0), ("o", -1), ("ffn0_stat", 3), ("ln_stat", 0), ("ffn0_yT", 2), ("x2", -1),
        ("ffn1_stat", -1), ("rstd", None), ("ln_norm", 0), ("ffn1_norm", -1), ("oT", -1), ("y2T", 0),
        ("ffn0_score", 2), ("ffn0_lo", 2), ("ffn0_head", 1), ("ffn1_yT", -1),
    ],
]
ENDING = [
    [
        "F", ("res1_T", -3), ("ffn1_score", -2),
        "F", ("scoreT", None),
        "F", ("kv", -1), ("mix", -1), ("ffn1_lo", -2), ("res1", -3), ("sigmoid", -1),
        "F",
        "F", ("gate", None), ("ffn1_combT", -2), ("gate2", None),
        "F", ("ffn1_head", -2), ("ev", -1),
        "F",
        "F", ("rcp0", -1), ("rcp1", -1), ("ffn0_norm", 2), ("rcp2", -1), ("rcp3", -1), ("r", -1), ("res0_T", 0),
        ("ffn0_combT", 1),
        "F", ("ffn0_score", 2),
        "F", ("wkv", -1), ("res0", 0), ("o", -1),
        "F", ("ln_stat", 0), ("ffn0_yT", 2), ("oT", -1),
        "F",
        "F", ("ffn0_stat", 3),
        "F", ("x2", -1), ("ffn1_stat", -1), ("rstd", None),
        "F", ("ln_norm", 0), ("ffn1_norm", -1), ("y2T", 0),
        "F", ("ffn1_yT", -1), ("ffn0_lo", 2), ("ffn0_head", 1),
    ],
    [
        ("ffn1_score", -2), ("res1_T", -3), ("mix", -1), ("ffn1_lo", -2), ("scoreT", None), ("gate", None),
        ("gate2", None), ("kv", -1), ("ev", -1), ("sigmoid", -1), ("ffn1_combT", -2), ("rcp0", -1), ("rcp1", -1),
        ("r", -1), ("rcp2", -1), ("ffn1_head", -2),
        "F", ("rcp3", -1), ("wkv", -1), ("o", -1), ("oT", -1), ("res1", -3),
        "F", "F",
        "F", ("x2", -1),
        "F", ("ffn1_stat", -1), ("rstd", None),
        "F", ("ffn1_norm", -1), ("ffn1_yT", -1),
        "F", "F",
    ],
    [
        ("ffn1_score", -2), ("ffn1_lo", -2), ("scoreT", None), ("gate", None), ("gate2", None), ("ffn1_combT", -2),
        ("res1_T", -3), ("ffn1_head", -2),
        "F", "F", "F", "F", "F",
        "F", ("res1", -3),
        "F", "F",
    ],
    [
        ("res1_T", -3), ("res1", -3),
    ],
]
SETUP = ("gate_w", "rows", "vectors", "w1", "b2_rows", "b2", "att_turn", "att_w", "first_z")
OFF = dict(item for item in SLOT if item != "F")
TR_USES = ("res1_T", "res0_T", "oT", "ffn0_yT", "y2T", "ffn1_yT")
SM_USES = ("ffn1_score", "scoreT", "ffn1_combT", "ffn0_combT", "ffn0_score")
SHARED = {"scoreT": (1, -2), "gate": (1, -2), "gate2": (1, -2), "rstd": (3, 0, -1)}
FIRST_SLOT = -3
GATE_STEPS = 15
RSTD_STEPS = 12
RSQRT_MAGIC = float(0x5F3759DF)
HEAD_TURNS = 2
TAIL_TURNS = 2
WRITTEN = 3


class Turn:

    def __init__(self, it=None):
        self.it = it

    def v(self, first, per):
        return first if self.it is None else self.it * per + (first - WRITTEN * per)


def macaron_kernel(nc, x, u, w, tmk, tmv, tmr, wk, wv, wr, wo, bo, gate_w, gate_b, w1, b1, w2, b2, out):
    B, T, D = x.shape
    E = w1.shape[0]
    UNITS = B * T // UNIT
    SLOTS = UNITS + 3
    assert D == P and w1.shape[2] == P and T == 2 * UNIT and UNITS % 2 == 0

    def exists(unit):
        return 0 <= unit < UNITS

    BLOCKS = [(f, s - 2 * f, e) for s in range(SLOTS) for f in range(2) if exists(s - 2 * f) for e in range(E)]
    FIRST = {(f, n): i for i, (f, n, e) in reversed(list(enumerate(BLOCKS))) if e == 0}
    PER = 4 * E
    HEAD = 2 * E

    def z_bank(n):
        return (n + 1) % Z_BANKS if n < HEAD else (n - HEAD) % PER % Z_BANKS

    def z_before(n):
        return next((k for k in range(n - 1, -1, -1) if z_bank(k) == z_bank(n)), None)

    def present(step, off, slot):
        if step in SETUP:
            return True
        if slot >= UNITS and off is not None and slot + off < UNITS + OFF[step]:
            return False
        return any(exists(slot + o) for o in (SHARED[step] if off is None else (off,)))

    def order(slot):
        if slot < FIRST_SLOT + len(OPENING):
            return OPENING[slot - FIRST_SLOT]
        return ENDING[slot - (SLOTS - len(ENDING))] if slot >= SLOTS - len(ENDING) else SLOT

    bank_uses = {names: [(step, t, off) for t in range(FIRST_SLOT, SLOTS)
                         for step, off in (item for item in order(t) if item[0] in names)
                         if present(step, off, t)] for names in (TR_USES, SM_USES)}
    use_no = {(step, t): k for names in bank_uses for k, (step, t, off) in enumerate(bank_uses[names])}

    def uses(step, slot):
        return use_no[step, slot]

    def last_use(names, step, slot):
        if use_no[step, slot] > 0:
            name, t, off = bank_uses[names][use_no[step, slot] - 1]
            return name, (t + off + 1 if off is not None else t + 2)

    x_u = x.rearrange("b (h c p) d -> (b h) p c d", c=TILES, p=P)
    out_u = out.rearrange("b (h c p) d -> (b h) p c d", c=TILES, p=P)

    with ExitStack() as ctx:
        def sb(name, shape, dt=F32):
            return ctx.enter_context(nc.sbuf_tensor(name, shape, dt))

        def sem(name):
            return ctx.enter_context(nc.semaphore(name))

        def bank(name):
            return ctx.enter_context(nc.psum_tensor(name, [P, UNIT], F32))

        ident = sb("ident", [P, P])
        w1_f = sb("w1_f", [P, E, P])
        w1_hi = sb("w1_hi", [P, E, P], F32R)
        w1_lo = sb("w1_lo", [P, E, P], F32R)
        w2_f = sb("w2_f", [P, E, P])
        gate_f = sb("gate_f", [P, E])
        gate_hi = sb("gate_hi", [P, P], F32R)
        gate_lo = sb("gate_lo", [P, P], F32R)
        gate_bias = sb("gate_bias", [E, 1])
        att_w = sb("att_w", [P, 4, P])
        att_wT = sb("att_wT", [P, 4, P])
        NV = 6 + E
        rows = sb("rows", [NV, P])
        cols = sb("cols", [P, NV])
        neg_b1 = sb("neg_b1", [P, E])
        u_minus_w = sb("u_minus_w", [P, 1])
        w_minus_u = sb("w_minus_u", [P, 1])
        neg_2w = sb("neg_2w", [P, 1])
        b1_diag = sb("b1_diag", [P, E, 3 * E])
        b2_f = sb("b2_f", [3 * E, P])
        b2_all = sb("b2_all", [3 * E, P])
        b2_hi = sb("b2_hi", [3 * E, P], F32R)
        b2_lo = sb("b2_lo", [3 * E, P])
        table_in = sb("table_in", [P, 1])
        table_out = sb("table_out", [P, 1])
        low_row = sb("low_row", [3 * E, 2])
        b2_mix = sb("b2_mix", [3 * E, P])
        b2_stack = sb("b2_stack", [3 * E, P], F32R)
        prio = sb("prio", [P, 2 * TILES, E])
        col = {name: cols[:, k:k + 1] for k, name in enumerate(["tmk", "tmv", "tmr", "u", "w", "bo"])}

        XL = sb("XL", [P, 2, TILES, P])
        X0 = sb("X0", [P, 2, TILES, P])
        X1 = sb("X1", [P, 2, TILES, P])
        X2 = sb("X2", [P, 2, TILES, P])
        OUT = sb("OUT", [P, 2, TILES, P])
        LN = ["ffn0", "ln", "ffn1"]
        st = {k: sb(f"st_{k}", [P, TILES, 6]) for k in LN}
        mv = sb("mv", [P, 3, TILES, 2])
        var_eps = sb("var_eps", [P, 3, TILES])
        rstd = sb("rstd", [P, 3, TILES])
        newton = sb("newton", [P, 3, TILES])
        shift = sb("shift", [P, 3, TILES])
        Y = {k: sb(f"Y_{k}", [P, TILES, P]) for k in LN}
        y_hi = [sb(f"y_hi{f}", [P, 2, UNIT], F32R) for f in range(2)]
        y_lo = [sb(f"y_lo{f}", [P, 2, UNIT], F32R) for f in range(2)]
        y_all = [sb(f"y_all{f}", [P, UNIT]) for f in range(2)]
        scT = sb("scT", [E, 2, UNIT])
        sc = sb("sc", [P, 2 * TILES, E])
        top = sb("top", [P, 2 * TILES])
        hit = sb("hit", [P, 2 * TILES, E])
        sel1 = sb("sel1", [P, 2 * TILES, E])
        rest = sb("rest", [P, 2 * TILES, E])
        sel2 = sb("sel2", [P, 2 * TILES, E])
        both = sb("both", [P, 2 * TILES, E])
        comb = sb("comb", [P, 2 * TILES, 3 * E])
        comb_hi = sb("comb_hi", [P, 2 * TILES, E], F32R)
        combT = [sb(f"combT{f}", [E, 2, UNIT]) for f in range(2)]
        comb_stack = [sb(f"comb_stack{f}", [3 * E, 2, UNIT], F32R) for f in range(2)]
        comb_row = sb("comb_row", [P, E * UNIT])
        BC = sb("BC", [P, BC_RING, UNIT])
        G = sb("G", [P, G_RING, UNIT])
        ffn_oT = [sb(f"ffn_oT{f}", [P, UNIT]) for f in range(2)]
        yT = sb("yT", [P, 1 + T])
        diff = sb("diff", [P, UNIT])
        key_in = sb("key_in", [P, UNIT])
        val_in = sb("val_in", [P, UNIT])
        rec_in = sb("rec_in", [P, UNIT])
        rec_t = sb("rec_t", [P, UNIT])
        rec_s = sb("rec_s", [P, UNIT])
        over = sb("over", [P, UNIT])
        under = sb("under", [P, UNIT])
        e1 = sb("e1", [P, UNIT])
        e2 = sb("e2", [P, UNIT])
        ev = sb("ev", [P, UNIT])
        A_ = sb("A_", [P, T])
        B_ = sb("B_", [P, T])
        rcp = sb("rcp", [P, UNIT])
        wkv = sb("wkv", [P, UNIT])
        wkvr = sb("wkvr", [P, UNIT])
        att_oT = sb("att_oT", [P, UNIT])

        Z = [bank(f"Z{k}") for k in range(Z_BANKS)]
        ACC = bank("ACC")
        TR = bank("TR")
        SM = bank("SM")
        KR = bank("KR")
        VO = bank("VO")

        s_w1 = sem("w1_in")
        s_w2 = sem("w2_in")
        s_small = sem("vectors_in")
        s_b1in = sem("b1_in")
        s_b2in = sem("b2_in")
        s_attw = sem("attw_in")
        s_gate = sem("gate_in")
        s_zero = sem("zeroed")
        s_ident = sem("ident_made")
        s_prio = sem("prio_made")
        s_rowsT = sem("rows_turned")
        s_cols = sem("cols_made")
        s_vec = sem("vectors_made")
        s_w1hi = sem("w1_hi_made")
        s_w1lo = sem("w1_lo_made")
        s_ghi = sem("gate_hi_made")
        s_glo = sem("gate_lo_made")
        s_wT = sem("att_w_turned")
        s_wTs = sem("att_wT_made")
        s_b2m = sem("b1_w2_made")
        s_b2 = sem("b2_steps")
        x_in = [sem(f"x_in{q}") for q in range(2)]
        xl_in = [sem(f"xl_in{q}") for q in range(2)]
        stats = {k: sem(f"stats_{k}") for k in LN}
        moments = {k: sem(f"moments_{k}") for k in LN}
        rstd_step = sem("rstd_step")
        normed = {k: sem(f"normed_{k}") for k in LN}
        tr_full = sem("tr_full")
        sm_full = sem("sm_full")
        sc_copied = sem("sc_copied")
        all_made = [sem(f"all_made{f}") for f in range(2)]
        hi_made = [sem(f"hi_made{f}") for f in range(2)]
        lo_made = [sem(f"lo_made{f}") for f in range(2)]
        scT_made = [sem(f"scT_made{f}") for f in range(2)]
        gate_step = sem("gate_step")
        combT_made = [sem(f"combT_made{f}") for f in range(2)]
        row_in = [[sem(f"row_in{f}{q}") for q in range(2)] for f in range(2)]
        bc_made = sem("bc_made")
        z_full = sem("z_full")
        g_made = sem("g_made")
        g_used = sem("g_used")
        acc_read = sem("acc_read")
        x1_made = sem("x1_made")
        x2_made = sem("x2_made")
        out_made = sem("out_made")
        out_done = [sem(f"out_done{q}") for q in range(2)]
        yT_made = sem("yT_made")
        diff_made = sem("diff_made")
        mixed = sem("mixed")
        tanh_made = sem("tanh_made")
        rec_made = sem("rec_made")
        k_full = sem("k_full")
        v_full = sem("v_full")
        r_full = sem("r_full")
        o_full = sem("o_full")
        over_made = sem("over_made")
        under_made = sem("under_made")
        e1_made = sem("e1_made")
        e2_made = sem("e2_made")
        ev_made = sem("ev_made")
        a_made = sem("a_made")
        b_made = sem("b_made")
        rcp_made = sem("rcp_made")
        wkv_made = sem("wkv_made")
        wkvr_made = sem("wkvr_made")
        o_read = sem("o_read")

        read_by = {"res1_T": out_made, "ffn0_yT": all_made[0], "res0_T": x1_made, "oT": x2_made, "y2T": yT_made,
                   "ffn1_yT": all_made[1], "ffn0_score": scT_made[0], "ffn1_score": scT_made[1],
                   "scoreT": sc_copied,
                   "ffn0_combT": combT_made[0], "ffn1_combT": combT_made[1]}

        def apart(eng):
            eng.sem_inc(waited, 1)

        waited = sem("waited")
        block = ctx.enter_context(nc.Block())

        def walk(steps, s, on_block):
            here = [n for n, (f, unit, e) in enumerate(BLOCKS) if unit + 2 * f == s]
            blocks = iter(here)
            for item in order(s):
                if item == "F":
                    n = next(blocks, None)
                    if n is not None:
                        on_block(n)
                    continue
                step, off = item
                if step in steps and present(step, off, s):
                    steps[step](s, s + off if off is not None else None)

        def pipeline(eng, before, one_slot):
            before()
            for s in range(FIRST_SLOT, 2 * HEAD_TURNS):
                one_slot(Turn(), s)
            with eng.Fori(HEAD_TURNS, UNITS // 2 - TAIL_TURNS) as it:
                for s in (2 * WRITTEN, 2 * WRITTEN + 1):
                    one_slot(Turn(it), s)
            for s in range(UNITS - 2 * TAIL_TURNS, SLOTS):
                one_slot(Turn(), s)

        @block.sync
        def _(sp):
            def load(t, unit, dst, done):
                src = x_u[t.v(unit, 2)] if t.it is not None else x_u[unit]
                sp.dma_start(dst[:, unit % 2], src).then_inc(done[unit % 2], 16)

            def one_slot(t, s):
                def ffn_row(f):
                    def step(s, unit):
                        q = unit % 2
                        sp.wait_ge(combT_made[f], t.v(unit + 1, 2))
                        apart(sp)
                        if unit >= 2:
                            sp.wait_ge(bc_made, t.v(FIRST[f, unit - 2] + E, PER))
                        at = 32 * (2 * f + q)
                        sp.dma_start(comb_row[at:at + 1].rearrange("p (e n) -> p e n", e=E),
                                     combT[f][:, q]).then_inc(row_in[f][q], 16)
                    return step

                def load_sum(s, unit):
                    if exists(unit + 2):
                        sp.wait_ge(x1_made, t.v(unit + 1, 2))
                        load(t, unit + 2, X0, x_in)

                def load_ln(s, unit):
                    if exists(unit + 2):
                        sp.wait_ge(normed["ffn0"], t.v(unit + 1, 2))
                        load(t, unit + 2, XL, xl_in)

                def store(s, unit):
                    q = unit % 2
                    sp.wait_ge(out_made, t.v(unit + 1, 2))
                    dst = out_u[t.v(unit, 2)] if t.it is not None else out_u[unit]
                    sp.dma_start(dst, OUT[:, q]).then_inc(out_done[q], 16)

                walk({"res0": load_sum, "ffn0_lo": load_ln, "res1": store, "ffn0_combT": ffn_row(0), "ffn1_combT": ffn_row(1)},
                     s, lambda n: None)

            def before():
                for q in range(2):
                    sp.sem_inc(out_done[q], 16)
                load(Turn(), 0, XL, xl_in)
                sp.dma_start(gate_f[:], gate_w).then_inc(s_gate, 16)
                sp.dma_start(gate_bias[:], gate_b.rearrange("(e a) -> e a", a=1)).then_inc(s_gate, 16)
                load(Turn(), 1, XL, xl_in)
                sp.dma_start(att_w[:, 0], wk).then_inc(s_attw, 16)
                sp.dma_start(att_w[:, 1], wv).then_inc(s_attw, 16)
                sp.dma_start(att_w[:, 2], wr).then_inc(s_attw, 16)
                sp.dma_start(att_w[:, 3], wo).then_inc(s_attw, 16)
                load(Turn(), 0, X0, x_in)
                load(Turn(), 1, X0, x_in)

            pipeline(sp, before, one_slot)
            for q in range(2):
                sp.wait_ge(out_done[q], 16 + 16 * UNITS // 2)

        @block.gpsimd
        def _(pool):
            def before():
                nc.gpsimd.memset(table_in[:], 0.0)
                nc.gpsimd.memset(ident[:], 0.0).then_inc(s_zero, 1)
                pool.wait_ge(s_zero, 1)
                for k, v in enumerate([tmk, tmv, tmr, u, w, bo]):
                    pool.dma_start(rows[k:k + 1, :], v.rearrange("(a d) -> a d", a=1)).then_inc(s_small, 16)
                nc.gpsimd.affine_select(out=ident[:], in_=ident[:], compare_op=ALU.not_equal, fill=1.0, base=0,
                                        pattern=[[-1, P]], channel_multiplier=1).then_inc(s_ident, 1)

            def broadcast(t, n):
                f, unit, e = BLOCKS[n]
                if e == 0:
                    pool.wait_ge(row_in[f][unit % 2], t.v(16 * (unit // 2 + 1), 16))
                if n >= BC_RING:
                    pool.wait_ge(g_made, t.v(n - BC_RING + 1, PER))
                apart(pool)
                at = 32 * (2 * f + unit % 2)
                nc.gpsimd.partition_broadcast(
                    BC[:, n % BC_RING], comb_row[at:at + 1, e * UNIT:(e + 1) * UNIT]).then_inc(bc_made, 1)

            def one_slot(t, s):
                def head(f):
                    def step(s, unit):
                        for e in range(BC_AHEAD):
                            broadcast(t, FIRST[f, unit] + e)
                    return step

                def on_block(n):
                    if BLOCKS[n][2] + BC_AHEAD < E:
                        broadcast(t, n + BC_AHEAD)

                walk({"ffn0_head": head(0), "ffn1_head": head(1)}, s, on_block)

            pipeline(pool, before, one_slot)

        @block.scalar
        def _(act):
            def before():
                act.dma_start(w1_f[:], w1.rearrange("e d h -> d e h")).then_inc(s_w1, 16)
                act.dma_start(rows[6:6 + E, :], b1).then_inc(s_b1in, 16)
                act.dma_start(w2_f[:], w2.rearrange("e h d -> h e d")).then_inc(s_w2, 16)
                for k in range(3):
                    act.dma_start(b2_f[k * E:(k + 1) * E, :], b2).then_inc(s_b2in, 16)
                act.wait_ge(s_zero, 1)
                nc.scalar.activation(table_out[:], table_in[:], ACT.Exp)

            def one_slot(t, s):
                def norm(k, X):
                    at = LN.index(k)

                    def step(s, unit):
                        made_in = unit - SHARED["rstd"][at]
                        act.wait_ge(rstd_step, t.v(RSTD_STEPS * (made_in - FIRST_SLOT + 1), 2 * RSTD_STEPS))
                        if unit >= 1:
                            yT_step = {"ffn0": "ffn0_yT", "ln": "y2T", "ffn1": "ffn1_yT"}[k]
                            act.wait_ge(tr_full, t.v(uses(yT_step, unit - 1 - OFF[yT_step]) + 1, 12))
                        for c in range(TILES):
                            last = nc.scalar.activation(Y[k][:, c], X[:, unit % 2, c], ACT.Identity,
                                                        bias=shift[:, at, c:c + 1], scale=rstd[:, at, c:c + 1])
                        last.then_inc(normed[k], 1)
                    return step

                def y_high(f):
                    def step(s, unit):
                        act.wait_ge(tr_full, t.v(uses(f"ffn{f}_yT", s) + 1, 12))
                        if unit >= 2:
                            act.wait_ge(z_full, t.v(FIRST[f, unit - 2] + E, PER))
                            act.wait_ge(sm_full, t.v(uses(f"ffn{f}_score", unit - 2 - OFF[f"ffn{f}_score"]) + 1, 10))
                        if unit >= 1:
                            act.wait_ge(lo_made[f], t.v(unit, 2))
                        nc.scalar.activation(y_all[f][:], TR[:], ACT.Copy).then_inc(all_made[f], 1)
                        act.wait_ge(all_made[f], t.v(unit + 1, 2))
                        nc.scalar.activation(y_hi[f][:, unit % 2], y_all[f][:], ACT.Copy).then_inc(hi_made[f], 1)
                    return step

                def score(f):
                    def step(s, unit):
                        n = uses(f"ffn{f}_score", s)
                        if unit == 0 and f == 0:
                            act.wait_ge(s_gate, 32)
                        act.wait_ge(sm_full, t.v(n + 1, 10))
                        nc.scalar.activation(scT[:, f], SM[0:E], ACT.Identity, bias=gate_bias[:, 0:1]).then_inc(scT_made[f], 1)
                    return step

                def comb_turned(f):
                    def step(s, unit):
                        act.wait_ge(sm_full, t.v(uses(f"ffn{f}_combT", s) + 1, 10))
                        if unit >= 2:
                            act.wait_ge(row_in[f][unit % 2], t.v(16 * (unit // 2), 16))
                            act.wait_ge(g_used, t.v(FIRST[f, unit - 2] + 1, PER))
                        nc.scalar.activation(comb_stack[f][:, unit % 2], SM[0:3 * E], ACT.Copy)
                        nc.scalar.activation(combT[f][:, unit % 2], SM[0:E], ACT.Copy).then_inc(combT_made[f], 1)
                    return step

                def y2_turned(s, unit):
                    lo = (unit % 2) * UNIT
                    act.wait_ge(tr_full, t.v(uses("y2T", s) + 1, 12))
                    if unit >= 1:
                        act.wait_ge(mixed, t.v(3 * unit, 6))
                    nc.scalar.activation(yT[:, lo + 1:lo + 1 + UNIT], TR[:], ACT.Copy).then_inc(yT_made, 1)

                def receptance(s, unit):
                    act.wait_ge(mixed, t.v(3 * unit + 1, 6))
                    if unit >= 1:
                        act.wait_ge(r_full, t.v(unit, 2))
                    nc.scalar.activation(rec_t[:], rec_in[:], ACT.Tanh, scale=0.5).then_inc(tanh_made, 1)
                    act.wait_ge(tanh_made, t.v(unit + 1, 2))
                    nc.scalar.activation(rec_s[:], rec_t[:], ACT.Copy, bias=0.5, scale=0.5).then_inc(rec_made, 1)

                def decays(s, unit):
                    if unit == 0:
                        act.wait_ge(s_vec, 4)
                    act.wait_ge(k_full, t.v(unit + 1, 2))
                    nc.scalar.activation(over[:], KR[:], ACT.Relu, bias=u_minus_w[:, 0:1]).then_inc(over_made, 1)
                    nc.scalar.activation(under[:], KR[:], ACT.Relu, bias=w_minus_u[:, 0:1], scale=-1.0).then_inc(under_made, 1)
                    act.wait_ge(over_made, t.v(unit + 1, 2))
                    if unit >= 1:
                        act.wait_ge(b_made, t.v(unit, 2))
                    nc.scalar.activation(e1[:], over[:], ACT.Exp, bias=neg_2w[:, 0:1], scale=-1.0).then_inc(e1_made, 1)
                    act.wait_ge(under_made, t.v(unit + 1, 2))
                    nc.scalar.activation(e2[:], under[:], ACT.Exp, scale=-1.0).then_inc(e2_made, 1)

                def att_out(s, unit):
                    act.wait_ge(o_full, t.v(unit + 1, 2))
                    if unit >= 1:
                        act.wait_ge(tr_full, t.v(uses("oT", unit - 1 - OFF["oT"]) + 1, 12))
                    nc.scalar.activation(att_oT[:], VO[:], ACT.Identity, bias=col["bo"]).then_inc(o_read, 1)

                def on_block(n):
                    f, unit, e = BLOCKS[n]
                    if e != E - 1:
                        return
                    act.wait_ge(g_used, t.v(n + 1, PER))
                    if unit >= 1:
                        act.wait_ge(tr_full, t.v(uses(f"res{f}_T", unit - 1 - OFF[f"res{f}_T"]) + 1, 12))
                    nc.scalar.activation(ffn_oT[f][:], ACC[:], ACT.Copy, scale=0.5).then_inc(acc_read, 1)

                walk({"ffn0_norm": norm("ffn0", XL), "ln_norm": norm("ln", X1), "ffn1_norm": norm("ffn1", X2),
                      "ffn0_yT": y_high(0), "ffn1_yT": y_high(1), "ffn0_score": score(0), "ffn1_score": score(1),
                      "ffn0_combT": comb_turned(0), "ffn1_combT": comb_turned(1), "y2T": y2_turned,
                      "sigmoid": receptance, "kv": decays, "o": att_out}, s, on_block)

            pipeline(act, before, one_slot)

        @block.vector
        def _(dve):
            def before():
                nc.vector.memset(yT[:, 0:1], 0.0)
                nc.vector.memset(b1_diag[:], 0.0)
                nc.vector.memset(mv[:], 1.0)
                nc.vector.memset(sc[:], 0.0)
                for e in range(E):
                    nc.vector.memset(prio[:, :, e:e + 1], float(E - e))
                nc.vector.memset(gate_hi[:].bitcast(F32), 0.0)
                nc.vector.memset(gate_lo[:].bitcast(F32), 0.0).then_inc(s_prio, 1)
                dve.wait_ge(s_prio, 1)

            def split_gate_w(s, unit):
                dve.wait_ge(s_gate, 32)
                nc.vector.tensor_copy(gate_hi[:, 0:E], gate_f[:]).then_inc(s_ghi, 1)
                dve.wait_ge(s_ghi, 1)
                nc.vector.tensor_tensor(gate_lo[:, 0:E], gate_f[:], gate_hi[:, 0:E].bitcast(F32),
                                        ALU.subtract).then_inc(s_glo, 1)

            def split_w1(s, unit):
                dve.wait_ge(s_w1, 16)
                nc.vector.tensor_copy(w1_hi[:], w1_f[:]).then_inc(s_w1hi, 1)
                dve.wait_ge(s_w1hi, 1)
                nc.vector.tensor_tensor(w1_lo[:], w1_f[:], w1_hi[:].bitcast(F32), ALU.subtract).then_inc(s_w1lo, 1)

            def vectors(s, unit):
                dve.wait_ge(s_rowsT, 1)
                nc.vector.tensor_copy(cols[:], KR[:, 0:NV]).then_inc(s_cols, 1)
                dve.wait_ge(s_cols, 1)
                nc.vector.tensor_scalar(neg_b1[:], cols[:, 6:NV], -1.0, None, ALU.mult).then_inc(s_vec, 1)
                nc.vector.tensor_tensor(u_minus_w[:], col["u"], col["w"], ALU.subtract).then_inc(s_vec, 1)
                nc.vector.tensor_tensor(w_minus_u[:], col["w"], col["u"], ALU.subtract).then_inc(s_vec, 1)
                nc.vector.tensor_scalar(neg_2w[:], col["w"], -2.0, None, ALU.mult).then_inc(s_vec, 1)
                diagonal = b1_diag[:].rearrange("p e n -> p (e n)")
                for k in range(3):
                    last = nc.vector.tensor_copy(diagonal[:, k * E::3 * E + 1], cols[:, 6:NV])
                last.then_inc(s_cols, 1)

            def stack_b2(s, unit):
                dve.wait_ge(s_b2m, 1)
                dve.wait_ge(s_b2in, 48)
                nc.vector.tensor_tensor(b2_all[:], VO[0:3 * E, 0:P], b2_f[:], ALU.add).then_inc(s_b2, 1)
                nc.vector.tensor_reduce(low_row[:, 0:1], ident[0:3 * E, 2 * E:3 * E], AX.X, ALU.add).then_inc(s_b2, 1)
                dve.wait_ge(s_b2, 2)
                nc.vector.tensor_copy(b2_hi[:], b2_all[:]).then_inc(s_b2, 1)
                nc.vector.tensor_scalar(low_row[:, 1:2], low_row[:, 0:1], -1.0, 1.0, ALU.mult, ALU.add).then_inc(s_b2, 1)
                dve.wait_ge(s_b2, 4)
                nc.vector.tensor_tensor(b2_lo[:], b2_all[:], b2_hi[:].bitcast(F32), ALU.subtract).then_inc(s_b2, 1)
                nc.vector.tensor_scalar(b2_mix[:], b2_hi[:].bitcast(F32), low_row[:, 1:2], None, ALU.mult).then_inc(s_b2, 1)
                dve.wait_ge(s_b2, 6)
                nc.vector.scalar_tensor_tensor(out=b2_stack[:], in0=b2_lo[:], scalar=low_row[:, 0:1], in1=b2_mix[:],
                                               op0=ALU.mult, op1=ALU.add).then_inc(s_b2, 1)

            def copy_att_w(s, unit):
                dve.wait_ge(s_wT, 1)
                nc.vector.tensor_copy(att_wT[:].rearrange("p a b -> p (a b)"), KR[:]).then_inc(s_wTs, 1)

            def one_slot(t, s):
                def stat(k, X):
                    at = LN.index(k)

                    def step(s, unit):
                        if k == "ffn0":
                            dve.wait_ge(xl_in[unit % 2], t.v(16 * (unit // 2 + 1), 16))
                        else:
                            dve.wait_ge({"ln": x1_made, "ffn1": x2_made}[k], t.v(unit + 1, 2))
                        for c in range(TILES):
                            last = nc.vector.bn_stats(st[k][:, c], X[:, unit % 2, c])
                        last.then_inc(stats[k], 1)
                        dve.wait_ge(stats[k], t.v(unit + 1, 2))
                        apart(dve)
                        for c in range(TILES):
                            last = nc.vector.bn_aggr(mv[:, at, c], st[k][:, c])
                        last.then_inc(moments[k], 1)
                    return step

                def rstd_all(s, unit):
                    turn_no = s - FIRST_SLOT
                    done = [0]

                    def then(ins):
                        done[0] += 1
                        ins.then_inc(rstd_step, 1)
                        dve.wait_ge(rstd_step, t.v(RSTD_STEPS * turn_no + done[0], 2 * RSTD_STEPS))

                    for k, off in zip(LN, SHARED["rstd"]):
                        if exists(s + off):
                            dve.wait_ge(moments[k], t.v(s + off + 1, 2))
                        if exists(s - 1 + off):
                            dve.wait_ge(normed[k], t.v(s + off, 2))
                    then(nc.vector.tensor_scalar(var_eps[:], mv[:, :, :, 1], LN_EPS, None, ALU.add))
                    then(nc.vector.tensor_scalar(rstd[:].bitcast(I32), var_eps[:].bitcast(I32), -0.5, RSQRT_MAGIC,
                                                 ALU.mult, ALU.add))
                    for _ in range(3):
                        then(nc.vector.tensor_tensor(newton[:], rstd[:], rstd[:], ALU.mult))
                        then(nc.vector.scalar_tensor_tensor(out=newton[:], in0=newton[:], scalar=-0.5, in1=var_eps[:],
                                                            op0=ALU.mult, op1=ALU.mult))
                        then(nc.vector.scalar_tensor_tensor(out=rstd[:], in0=newton[:], scalar=1.5, in1=rstd[:],
                                                            op0=ALU.add, op1=ALU.mult))
                    then(nc.vector.scalar_tensor_tensor(out=shift[:], in0=mv[:, :, :, 0], scalar=-1.0, in1=rstd[:],
                                                        op0=ALU.mult, op1=ALU.mult))
                    assert done[0] == RSTD_STEPS

                def y_low(f):
                    def step(s, unit):
                        dve.wait_ge(hi_made[f], t.v(unit + 1, 2))
                        nc.vector.tensor_tensor(y_lo[f][:, unit % 2], y_all[f][:], y_hi[f][:, unit % 2].bitcast(F32),
                                                ALU.subtract).then_inc(lo_made[f], 1)
                    return step

                def wide(a):
                    return a[:].unsqueeze(2).to_broadcast([P, 2 * TILES, E])

                def gate_then(s, before):
                    done = [before]

                    def then(ins, n=1):
                        done[0] += n
                        ins.then_inc(gate_step, 1)
                        dve.wait_ge(gate_step, t.v(GATE_STEPS * (s + 1) + done[0], 2 * GATE_STEPS))
                    return then

                def gate(s, unit):
                    turn_no = s + 1
                    then = gate_then(s, 0)
                    has = [exists(s + off) for off in SHARED["gate"]]
                    lo, hi = (0 if has[0] else TILES), (2 * TILES if has[1] else TILES)
                    dve.wait_ge(sm_full, t.v(uses("scoreT", s) + 1, 10))
                    nc.vector.tensor_copy(sc[:, lo:hi].rearrange("p c e -> p (c e)"), SM[:, lo * E:hi * E]).then_inc(sc_copied, 1)
                    dve.wait_ge(sc_copied, t.v(turn_no + 1, 2))
                    then(nc.vector.tensor_reduce(top[:], sc[:], AX.X, ALU.max))
                    then(nc.vector.tensor_tensor(hit[:], sc[:], wide(top), ALU.is_equal))
                    then(nc.vector.tensor_tensor(hit[:], hit[:], prio[:], ALU.mult))
                    then(nc.vector.tensor_reduce(top[:], hit[:], AX.X, ALU.max))
                    then(nc.vector.tensor_tensor(sel1[:], hit[:], wide(top), ALU.is_equal))
                    then(nc.vector.scalar_tensor_tensor(out=rest[:], in0=sel1[:], scalar=-3.0e38, in1=sc[:],
                                                        op0=ALU.mult, op1=ALU.add))

                def gate2(s, unit):
                    then = gate_then(s, 6)
                    then(nc.vector.tensor_reduce(top[:], rest[:], AX.X, ALU.max))
                    then(nc.vector.tensor_tensor(hit[:], rest[:], wide(top), ALU.is_equal))
                    then(nc.vector.tensor_tensor(hit[:], hit[:], prio[:], ALU.mult))
                    then(nc.vector.tensor_reduce(top[:], hit[:], AX.X, ALU.max))
                    then(nc.vector.tensor_tensor(sel2[:], hit[:], wide(top), ALU.is_equal))
                    then(nc.vector.tensor_tensor(both[:], sel1[:], sel2[:], ALU.add))
                    nc.vector.tensor_tensor(comb[:, :, 0:E], both[:], sc[:], ALU.mult).then_inc(gate_step, 1)
                    nc.vector.tensor_tensor(comb[:, :, 2 * E:3 * E], both[:], sc[:], ALU.mult)
                    then(nc.vector.tensor_tensor(comb_hi[:], both[:], sc[:], ALU.mult), 2)
                    nc.vector.tensor_tensor(comb[:, :, E:2 * E], comb[:, :, 0:E], comb_hi[:].bitcast(F32),
                                            ALU.subtract).then_inc(gate_step, 1)

                def residual(name, src, dst, made):
                    def step(s, unit):
                        q = unit % 2
                        n = uses(name, s)
                        dve.wait_ge(tr_full, t.v(n + 1, 12))
                        if name == "res0_T":
                            dve.wait_ge(x_in[q], t.v(16 * (unit // 2 + 1), 16))
                        if name == "res1_T" and unit >= 2:
                            dve.wait_ge(out_done[q], t.v(16 + 16 * (unit // 2), 16))
                        nc.vector.tensor_tensor(dst[:, q].rearrange("p c d -> p (c d)"),
                                                src[:, q].rearrange("p c d -> p (c d)"), TR[:], ALU.add).then_inc(made, 1)
                    return step

                def mix(s, unit):
                    lo = (unit % 2) * UNIT
                    dve.wait_ge(yT_made, t.v(unit + 1, 2))
                    nc.vector.tensor_tensor(diff[:], yT[:, lo + 1:lo + 1 + UNIT], yT[:, lo:lo + UNIT],
                                            ALU.subtract).then_inc(diff_made, 1)
                    dve.wait_ge(diff_made, t.v(unit + 1, 2))
                    if unit >= 1:
                        dve.wait_ge(v_full, t.v(unit, 2))
                        dve.wait_ge(tanh_made, t.v(unit, 2))
                    for name, dst in (("tmr", rec_in), ("tmk", key_in), ("tmv", val_in)):
                        nc.vector.scalar_tensor_tensor(out=dst[:], in0=diff[:], scalar=col[name], in1=yT[:, lo:lo + UNIT],
                                                       op0=ALU.mult, op1=ALU.add).then_inc(mixed, 1)

                def scans(s, unit):
                    lo = (unit % 2) * UNIT
                    dve.wait_ge(e2_made, t.v(unit + 1, 2))
                    dve.wait_ge(v_full, t.v(unit + 1, 2))
                    nc.vector.tensor_tensor(ev[:], VO[:], e2[:], ALU.mult).then_inc(ev_made, 1)
                    first = unit % 2 == 0
                    if not first:
                        dve.wait_ge(b_made, t.v(unit, 2))
                    nc.vector.tensor_tensor_scan(B_[:, lo:lo + UNIT], e1[:], e2[:], 0.0 if first else B_[:, lo - 1:lo],
                                                 ALU.mult, ALU.add).then_inc(b_made, 1)
                    dve.wait_ge(ev_made, t.v(unit + 1, 2))
                    nc.vector.tensor_tensor_scan(A_[:, lo:lo + UNIT], e1[:], ev[:], 0.0 if first else A_[:, lo - 1:lo],
                                                 ALU.mult, ALU.add).then_inc(a_made, 1)

                def rcp_part(k):
                    def step(s, unit):
                        lo = (unit % 2) * UNIT
                        if k == 0:
                            dve.wait_ge(b_made, t.v(unit + 1, 2))
                        nc.vector.reciprocal(rcp[:, k * P:(k + 1) * P], B_[:, lo + k * P:lo + (k + 1) * P]).then_inc(rcp_made, 1)
                    return step

                def weigh(s, unit):
                    lo = (unit % 2) * UNIT
                    dve.wait_ge(rcp_made, t.v(TILES * (unit + 1), 2 * TILES))
                    dve.wait_ge(a_made, t.v(unit + 1, 2))
                    nc.vector.tensor_tensor(wkv[:], A_[:, lo:lo + UNIT], rcp[:], ALU.mult).then_inc(wkv_made, 1)
                    dve.wait_ge(wkv_made, t.v(unit + 1, 2))
                    dve.wait_ge(r_full, t.v(unit + 1, 2))
                    if unit >= 1:
                        dve.wait_ge(o_full, t.v(unit, 2))
                    nc.vector.tensor_tensor(wkvr[:], KR[:], wkv[:], ALU.mult).then_inc(wkvr_made, 1)

                def on_block(n):
                    f, unit, e = BLOCKS[n]
                    dve.wait_ge(z_full, t.v(n + 1, PER))
                    dve.wait_ge(bc_made, t.v(n + 1, PER))
                    if n >= G_RING:
                        dve.wait_ge(g_used, t.v(n - G_RING + 1, PER))
                    nc.vector.scalar_tensor_tensor(out=G[:, n % G_RING], in0=Z[z_bank(n)][:], scalar=neg_b1[:, e:e + 1],
                                                   in1=BC[:, n % BC_RING], op0=ALU.max, op1=ALU.mult).then_inc(g_made, 1)

                steps = {"ffn0_stat": stat("ffn0", XL), "ln_stat": stat("ln", X1), "ffn1_stat": stat("ffn1", X2),
                         "ffn0_lo": y_low(0), "ffn1_lo": y_low(1), "gate": gate, "gate2": gate2, "rstd": rstd_all,
                         "res0": residual("res0_T", X0, X1, x1_made), "x2": residual("oT", X1, X2, x2_made),
                         "res1": residual("res1_T", X2, OUT, out_made), "mix": mix, "ev": scans, "wkv": weigh}
                steps |= {f"rcp{k}": rcp_part(k) for k in range(TILES)}
                steps |= {"gate_w": split_gate_w, "w1": split_w1, "vectors": vectors, "b2": stack_b2, "att_w": copy_att_w}
                walk(steps, s, on_block)

            pipeline(dve, before, one_slot)

        @block.tensor
        def _(pe):
            def before():
                pe.wait_ge(s_ident, 1)

            def turn_rows(s, unit):
                pe.wait_ge(s_small, 16 * 6)
                pe.wait_ge(s_b1in, 16)
                nc.tensor.transpose(KR[:, 0:NV], rows[:], ident[0:NV, 0:NV]).then_inc(s_rowsT, 1)

            def b1_w2(s, unit):
                pe.wait_ge(s_w2, 16)
                pe.wait_ge(s_cols, 2)
                for e in range(E):
                    last = nc.tensor.matmul(VO[0:3 * E, 0:P], b1_diag[:, e], w2_f[:, e], start=(e == 0), stop=(e == E - 1))
                last.then_inc(s_b2m, 1)

            def turn_att_w(s, unit):
                pe.wait_ge(s_cols, 1)
                pe.wait_ge(s_attw, 64)
                for k in range(4):
                    last = nc.tensor.transpose(KR[:, k * P:(k + 1) * P], att_w[:, k], ident[:])
                last.then_inc(s_wT, 1)

            def first_z(s, unit):
                pe.wait_ge(s_w1lo, 1)
                for n in range(Z_AHEAD):
                    up(Turn(), n)

            def up(t, n):
                f, unit, e = BLOCKS[n]
                if e == 0:
                    pe.wait_ge(lo_made[f], t.v(unit + 1, 2))
                if (k := z_before(n)) is not None:
                    pe.wait_ge(g_made, t.v(k + 1, PER))
                z = Z[z_bank(n)][:]
                q = unit % 2
                nc.tensor.matmul(z, w1_hi[:, e], y_hi[f][:, q], start=True, stop=False)
                nc.tensor.matmul(z, w1_hi[:, e], y_lo[f][:, q], start=False, stop=False)
                nc.tensor.matmul(z, w1_lo[:, e], y_hi[f][:, q], start=False, stop=True).then_inc(z_full, 1)

            def down(t, n):
                f, unit, e = BLOCKS[n]
                if e == 0:
                    if n >= E:
                        pe.wait_ge(acc_read, t.v(n // E, 4))
                    pe.wait_ge(combT_made[f], t.v(unit + 1, 2))
                    if n == 0:
                        pe.wait_ge(s_b2, 7)
                    nc.tensor.matmul(ACC[:], b2_stack[:], comb_stack[f][:, unit % 2], start=True, stop=False)
                pe.wait_ge(g_made, t.v(n + 1, PER))
                last = nc.tensor.matmul(ACC[:], w2_f[:, e], G[:, n % G_RING], start=False, stop=(e == E - 1))
                last.then_inc(g_used, 1)

            def one_slot(t, s):
                def bank_read(table, step, s):
                    if (past := last_use(table, step, s)) is not None:
                        pe.wait_ge(read_by[past[0]], t.v(past[1], 2))

                def turn(step_name, source, wait):
                    def step(s, unit):
                        bank_read(TR_USES, step_name, s)
                        wait(unit)
                        for c in range(TILES):
                            last = nc.tensor.transpose(TR[:, c * P:(c + 1) * P], source(c), ident[:])
                        last.then_inc(tr_full, 1)
                    return step

                def y_turn(name, k):
                    return turn(name, lambda c: Y[k][:, c], lambda unit: pe.wait_ge(normed[k], t.v(unit + 1, 2)))

                def ffn_turn(f):
                    return turn(f"res{f}_T", lambda c: ffn_oT[f][:, c * P:(c + 1) * P],
                                lambda unit: pe.wait_ge(acc_read, t.v(FIRST[f, unit] // E + 1, 4)))

                def score(f):
                    def step(s, unit):
                        bank_read(SM_USES, f"ffn{f}_score", s)
                        pe.wait_ge(lo_made[f], t.v(unit + 1, 2))
                        if unit == 0 and f == 0:
                            pe.wait_ge(s_glo, 1)
                        q = unit % 2
                        nc.tensor.matmul(SM[:], gate_hi[:], y_hi[f][:, q], start=True, stop=False)
                        nc.tensor.matmul(SM[:], gate_hi[:], y_lo[f][:, q], start=False, stop=False)
                        nc.tensor.matmul(SM[:], gate_lo[:], y_hi[f][:, q], start=False, stop=True).then_inc(sm_full, 1)
                    return step

                def scores_back(s, unit):
                    bank_read(SM_USES, "scoreT", s)
                    for f, off in enumerate(SHARED["scoreT"]):
                        if exists(s + off):
                            pe.wait_ge(scT_made[f], t.v(s + off + 1, 2))
                            apart(pe)
                            for c in range(TILES):
                                at = (f * TILES + c) * E
                                last = nc.tensor.transpose(SM[:, at:at + E], scT[:, f, c * P:(c + 1) * P], ident[0:E, 0:E])
                    last.then_inc(sm_full, 1)

                def comb_turn(f):
                    def step(s, unit):
                        bank_read(SM_USES, f"ffn{f}_combT", s)
                        pe.wait_ge(gate_step, t.v(GATE_STEPS * (s + 2), 2 * GATE_STEPS))
                        for c in range(TILES):
                            last = nc.tensor.transpose(SM[0:3 * E, c * P:(c + 1) * P], comb[:, f * TILES + c], ident[:])
                        last.then_inc(sm_full, 1)
                    return step

                def keys_values(s, unit):
                    if unit == 0:
                        pe.wait_ge(s_wTs, 1)
                    pe.wait_ge(mixed, t.v(3 * (unit + 1), 6))
                    if unit >= 1:
                        pe.wait_ge(wkvr_made, t.v(unit, 2))
                        pe.wait_ge(o_read, t.v(unit, 2))
                    nc.tensor.matmul(KR[:], att_wT[:, 0], key_in[:], start=True, stop=True).then_inc(k_full, 1)
                    nc.tensor.matmul(VO[:], att_wT[:, 1], val_in[:], start=True, stop=True).then_inc(v_full, 1)

                def receptance(s, unit):
                    pe.wait_ge(under_made, t.v(unit + 1, 2))
                    pe.wait_ge(rec_made, t.v(unit + 1, 2))
                    nc.tensor.matmul(KR[:], att_wT[:, 2], rec_s[:], start=True, stop=True).then_inc(r_full, 1)

                def output(s, unit):
                    pe.wait_ge(ev_made, t.v(unit + 1, 2))
                    pe.wait_ge(wkvr_made, t.v(unit + 1, 2))
                    nc.tensor.matmul(VO[:], att_wT[:, 3], wkvr[:], start=True, stop=True).then_inc(o_full, 1)

                def late(unit, f):
                    return unit + 2 * f >= UNITS

                def head(s, unit):
                    if late(unit, 1):
                        for e in range(Z_AHEAD):
                            up(t, FIRST[1, unit] + e)

                def on_block(n):
                    if n + Z_AHEAD < len(BLOCKS):
                        f, unit, e = BLOCKS[n + Z_AHEAD]
                        if not (late(unit, f) and e < Z_AHEAD):
                            up(t, n + Z_AHEAD)
                    down(t, n)

                walk({"res0_T": ffn_turn(0), "res1_T": ffn_turn(1), "ffn0_yT": y_turn("ffn0_yT", "ffn0"),
                      "y2T": y_turn("y2T", "ln"), "ffn1_yT": y_turn("ffn1_yT", "ffn1"),
                      "oT": turn("oT", lambda c: att_oT[:, c * P:(c + 1) * P], lambda unit: pe.wait_ge(o_read, t.v(unit + 1, 2))),
                      "ffn0_score": score(0), "ffn1_score": score(1), "scoreT": scores_back,
                      "ffn0_combT": comb_turn(0), "ffn1_combT": comb_turn(1),
                      "kv": keys_values, "r": receptance, "o": output, "ffn1_head": head,
                      "rows": turn_rows, "b2_rows": b1_w2, "att_turn": turn_att_w, "first_z": first_z}, s, on_block)

            pipeline(pe, before, one_slot)


_INS = ['L0_attn_x', 'L0_attn_u', 'L0_attn_w', 'L0_attn_tmk', 'L0_attn_tmv', 'L0_attn_tmr', 'L0_attn_Wk', 'L0_attn_Wv',
        'L0_attn_Wr', 'L0_attn_Wo', 'L0_attn_bo', 'L0_ffn_gate_w', 'L0_ffn_gate_b', 'L0_ffn_w1', 'L0_ffn_b1',
        'L0_ffn_w2', 'L0_ffn_b2']


def kernel(**inputs):
    import numpy as np
    import concourse.bacc as bacc
    from concourse.bass_utils import run_bass_kernel_spmd

    nc = bacc.Bacc("TRN2", target_bir_lowering=False, num_devices=1)
    arrays, args = {}, []
    for name in _INS:
        a = np.ascontiguousarray(inputs[name])
        arrays[f"in_{name}"] = a
        args.append(nc.dram_tensor(f"in_{name}", a.shape, mybir.dt.from_np(a.dtype), kind="ExternalInput").ap())
    shape = inputs["L0_attn_x"].shape
    out = nc.dram_tensor("out", shape, F32, kind="ExternalOutput").ap()
    macaron_kernel(nc, *args, out)
    r = run_bass_kernel_spmd(nc, [arrays], core_ids=[0])
    return r.results[0]["out"]
```

```python
from contextlib import ExitStack

import concourse.bass as bass
from concourse import mybir

P = 128
F32 = mybir.dt.float32
F32R = mybir.dt.float32r
I32 = mybir.dt.int32
ALU = mybir.AluOpType
ACT = mybir.ActivationFunctionType
AX = mybir.AxisListType

UNIT = 512
TILES = UNIT // P
LN_EPS = 1e-5
Z_BANKS = 3
G_RING = 4
BC_RING = 8
BC_AHEAD = 4
Z_AHEAD = 3

SLOT = [
    "F", ("res1_T", -3), ("ffn0_norm", 2), ("ffn1_score", -2),
    "F", ("scoreT", None),
    "F", ("kv", -1), ("mix", -1), ("ffn1_lo", -2), ("ffn0_stat", 3),
    "F", ("res1", -3),
    "F", ("gate0", None), ("gate1", None), ("gate2", None), ("ffn1_combT", -2), ("ffn0_yT", 2), ("gate3", None),
    ("gate4", None), ("gate5", None), ("gate6", None), ("gate7", None), ("ffn1_head", -2), ("gate8", None),
    ("gate9", None), ("gate10", None), ("gate11", None), ("gate12", None),
    "F", ("gate13", None),
    "F", ("gate14", None), ("ev", -1), ("sigmoid", -1), ("rcp0", -1), ("rcp1", -1),
    "F", ("r", -1), ("res0_T", 0), ("rcp2", -1), ("rcp3", -1),
    "F", ("wkv", -1), ("o", -1), ("res0", 0),
    "F", ("oT", -1),
    "F", ("ln_stat", 0),
    "F", ("ffn0_combT", 1), ("x2", -1), ("ffn1_stat", -1), ("rstd0", None),
    "F", ("rstd1", None), ("rstd2", None), ("rstd3", None), ("rstd4", None), ("rstd5", None),
    "F", ("rstd6", None),
    "F", ("rstd7", None), ("rstd8", None), ("rstd9", None), ("rstd10", None), ("rstd11", None), ("ln_norm", 0),
    ("ffn1_norm", -1), ("y2T", 0),
    "F", ("ffn1_yT", -1), ("ffn0_score", 2), ("ffn0_head", 1), ("ffn0_lo", 2),
]
OPENING = [
    [
        ("ffn0_stat", 3), ("rstd0", None), ("rstd1", None), ("rstd2", None), ("rstd3", None), ("rstd4", None),
        ("rstd5", None), ("rstd6", None), ("rstd7", None), ("rstd8", None), ("rstd9", None), ("rstd10", None),
        ("rstd11", None),
    ],
    [
        ("ffn0_stat", 3), ("vectors", None), ("rstd0", None), ("rstd1", None), ("rows", None), ("rstd2", None),
        ("gate_w", None), ("rstd3", None), ("w1", None), ("rstd4", None), ("rstd5", None), ("rstd6", None),
        ("ffn0_norm", 2), ("rstd7", None), ("ffn0_yT", 2), ("rstd8", None), ("ffn0_lo", 2), ("b2_rows", None),
        ("rstd9", None), ("ffn0_score", 2), ("rstd10", None), ("rstd11", None),
    ],
    [
        ("scoreT", None), ("ffn0_stat", 3), ("ffn0_norm", 2), ("gate0", None), ("gate1", None), ("gate2", None),
        ("gate3", None), ("gate4", None), ("gate5", None), ("ffn0_yT", 2), ("gate6", None), ("gate7", None),
        ("att_turn", None), ("gate8", None), ("gate9", None), ("gate10", None), ("gate11", None), ("gate12", None),
        ("gate13", None), ("gate14", None), ("ffn0_lo", 2), ("ffn0_combT", 1), ("rstd0", None), ("rstd1", None),
        ("ffn0_score", 2), ("rstd2", None), ("rstd3", None), ("b2", None), ("rstd4", None), ("rstd5", None),
        ("ffn0_head", 1), ("first_z", None), ("rstd6", None), ("rstd7", None), ("rstd8", None), ("rstd9", None),
        ("rstd10", None), ("rstd11", None),
    ],
    [
        ("ffn0_norm", 2),
        "F", "F", "F",
        "F", ("scoreT", None),
        "F", "F",
        "F", ("gate0", None), ("att_w", None), ("gate1", None),
        "F", ("ffn0_combT", 1), ("gate2", None), ("gate3", None), ("gate4", None), ("gate5", None), ("gate6", None),
        ("gate7", None), ("gate8", None), ("gate9", None), ("gate10", None), ("gate11", None), ("gate12", None),
        ("gate13", None), ("gate14", None), ("ffn0_stat", 3), ("res0", 0), ("ln_stat", 0), ("rstd0", None),
        ("rstd1", None), ("rstd2", None), ("rstd3", None), ("rstd4", None), ("rstd5", None), ("rstd6", None),
        ("rstd7", None), ("rstd8", None), ("rstd9", None), ("rstd10", None), ("rstd11", None), ("ffn0_head", 1),
        ("res0_T", 0), ("ffn0_yT", 2), ("ln_norm", 0), ("ffn0_lo", 2), ("ffn0_score", 2), ("y2T", 0),
    ],
    [
        ("sigmoid", -1),
        "F",
        "F", ("scoreT", None),
        "F",
        "F", ("mix", -1), ("kv", -1), ("gate0", None), ("gate1", None), ("gate2", None), ("gate3", None),
        ("gate4", None), ("gate5", None),
        "F", ("gate6", None), ("gate7", None), ("gate8", None), ("r", -1), ("ffn0_norm", 2),
        "F", ("gate9", None), ("gate10", None),
        "F", ("gate11", None), ("gate12", None),
        "F", ("ev", -1), ("gate13", None), ("rcp0", -1), ("rcp1", -1), ("rcp2", -1), ("res0_T", 0), ("rcp3", -1),
        ("gate14", None), ("wkv", -1), ("ffn0_combT", 1), ("res0", 0), ("o", -1), ("ln_stat", 0), ("ffn0_stat", 3),
        ("ffn0_yT", 2), ("x2", -1), ("ffn1_stat", -1), ("rstd0", None), ("rstd1", None), ("rstd2", None),
        ("rstd3", None), ("rstd4", None), ("rstd5", None), ("rstd6", None), ("rstd7", None), ("rstd8", None),
        ("rstd9", None), ("rstd10", None), ("rstd11", None), ("ln_norm", 0), ("ffn0_lo", 2), ("ffn1_norm", -1),
        ("oT", -1), ("y2T", 0), ("ffn0_score", 2), ("ffn1_yT", -1), ("ffn0_head", 1),
    ],
]
ENDING = [
    [
        "F", ("res1_T", -3), ("ffn1_score", -2),
        "F", ("scoreT", None),
        "F", ("kv", -1), ("mix", -1), ("ffn1_lo", -2),
        "F", ("res1", -3),
        "F", ("gate0", None), ("sigmoid", -1), ("gate1", None), ("gate2", None), ("ffn1_combT", -2),
        ("gate3", None), ("gate4", None), ("gate5", None), ("gate6", None), ("gate7", None), ("gate8", None),
        ("gate9", None),
        "F", ("gate10", None), ("gate11", None), ("gate12", None), ("gate13", None), ("ffn0_norm", 2),
        "F", ("gate14", None), ("ev", -1),
        "F", ("rcp0", -1), ("rcp1", -1), ("rcp2", -1), ("rcp3", -1), ("r", -1), ("ffn1_head", -2), ("res0_T", 0),
        "F", ("wkv", -1), ("ffn0_yT", 2), ("o", -1),
        "F",
        "F", ("ffn0_combT", 1), ("res0", 0), ("oT", -1), ("ffn0_score", 2), ("ln_stat", 0),
        "F",
        "F", ("ffn0_stat", 3),
        "F", ("x2", -1), ("ffn1_stat", -1), ("rstd0", None), ("rstd1", None), ("rstd2", None), ("rstd3", None),
        ("rstd4", None), ("rstd5", None), ("rstd6", None), ("rstd7", None), ("rstd8", None), ("rstd9", None),
        ("rstd10", None), ("rstd11", None), ("ln_norm", 0), ("ffn0_head", 1),
        "F", ("ffn1_norm", -1), ("y2T", 0),
        "F", ("ffn0_lo", 2), ("ffn1_yT", -1),
    ],
    [
        ("mix", -1), ("ffn1_lo", -2), ("res1_T", -3), ("ffn1_score", -2), ("scoreT", None), ("gate0", None),
        ("gate1", None), ("gate2", None), ("gate3", None), ("gate4", None), ("gate5", None), ("gate6", None),
        ("gate7", None), ("gate8", None), ("gate9", None), ("gate10", None), ("gate11", None), ("gate12", None),
        ("gate13", None), ("gate14", None), ("kv", -1), ("ev", -1), ("ffn1_combT", -2), ("ffn1_head", -2),
        ("rcp0", -1), ("sigmoid", -1), ("r", -1), ("rcp1", -1), ("rcp2", -1),
        "F", ("rcp3", -1), ("o", -1), ("oT", -1), ("wkv", -1), ("res1", -3),
        "F", "F",
        "F", ("x2", -1), ("ffn1_stat", -1),
        "F", ("rstd0", None), ("rstd1", None), ("rstd2", None), ("rstd3", None), ("rstd4", None), ("rstd5", None),
        ("rstd6", None), ("rstd7", None), ("rstd8", None), ("rstd9", None), ("rstd10", None), ("rstd11", None),
        "F", ("ffn1_norm", -1), ("ffn1_yT", -1),
        "F", "F",
    ],
    [
        ("ffn1_score", -2), ("scoreT", None), ("ffn1_lo", -2), ("gate0", None), ("gate1", None), ("gate2", None),
        ("gate3", None), ("gate4", None), ("gate5", None), ("gate6", None), ("gate7", None), ("gate8", None),
        ("gate9", None), ("gate10", None), ("gate11", None), ("res1_T", -3), ("gate12", None), ("ffn1_combT", -2),
        ("gate13", None), ("gate14", None), ("ffn1_head", -2),
        "F", "F", "F", "F", "F",
        "F", ("res1", -3),
        "F", "F",
    ],
    [
        ("res1_T", -3), ("res1", -3),
    ],
]
SETUP = ("gate_w", "rows", "vectors", "w1", "b2_rows", "b2", "att_turn", "att_w", "first_z")
OFF = dict(item for item in SLOT if item != "F")
TR_USES = ("res1_T", "res0_T", "oT", "ffn0_yT", "y2T", "ffn1_yT")
SM_USES = ("ffn1_score", "scoreT", "ffn1_combT", "ffn0_combT", "ffn0_score")
GATE_STEPS = 15
GATE_PARTS = 15
RSTD_STEPS = 12
TR_PER = 2 * len(TR_USES)
SM_PER = 2 * len(SM_USES)
SHARED = {"scoreT": (1, -2)}
SHARED |= {f"gate{k}": (1, -2) for k in range(GATE_PARTS)} | {f"rstd{k}": (3, 0, -1) for k in range(RSTD_STEPS)}
FIRST_SLOT = -3
RSQRT_MAGIC = float(0x5F3759DF)
HEAD_TURNS = 2
TAIL_TURNS = 2
WRITTEN = 3


class Turn:

    def __init__(self, it=None):
        self.it = it

    def v(self, first, per):
        return first if self.it is None else self.it * per + (first - WRITTEN * per)


def macaron_kernel(nc, x, u, w, tmk, tmv, tmr, wk, wv, wr, wo, bo, gate_w, gate_b, w1, b1, w2, b2, out):
    B, T, D = x.shape
    E = w1.shape[0]
    UNITS = B * T // UNIT
    SLOTS = UNITS + 3
    assert D == P and w1.shape[2] == P and T == 2 * UNIT and UNITS % 2 == 0

    def exists(unit):
        return 0 <= unit < UNITS

    BLOCKS = [(f, s - 2 * f, e) for s in range(SLOTS) for f in range(2) if exists(s - 2 * f) for e in range(E)]
    FIRST = {(f, n): i for i, (f, n, e) in reversed(list(enumerate(BLOCKS))) if e == 0}
    PER = 4 * E
    HEAD = 2 * E

    def z_bank(n):
        return (n + 1) % Z_BANKS if n < HEAD else (n - HEAD) % PER % Z_BANKS

    def z_before(n):
        return next((k for k in range(n - 1, -1, -1) if z_bank(k) == z_bank(n)), None)

    def present(step, off, slot):
        if step in SETUP:
            return True
        if slot >= UNITS and off is not None and slot + off < UNITS + OFF[step]:
            return False
        return any(exists(slot + o) for o in (SHARED[step] if off is None else (off,)))

    def order(slot):
        if slot < FIRST_SLOT + len(OPENING):
            return OPENING[slot - FIRST_SLOT]
        return ENDING[slot - (SLOTS - len(ENDING))] if slot >= SLOTS - len(ENDING) else SLOT

    bank_uses = {names: [(step, t, off) for t in range(FIRST_SLOT, SLOTS)
                         for step, off in (item for item in order(t) if item[0] in names)
                         if present(step, off, t)] for names in (TR_USES, SM_USES)}
    use_no = {(step, t): k for names in bank_uses for k, (step, t, off) in enumerate(bank_uses[names])}

    def uses(step, slot):
        return use_no[step, slot]

    def last_use(names, step, slot):
        if use_no[step, slot] > 0:
            name, t, off = bank_uses[names][use_no[step, slot] - 1]
            return name, (t + off + 1 if off is not None else t + 2)

    x_u = x.rearrange("b (h c p) d -> (b h) p c d", c=TILES, p=P)
    out_u = out.rearrange("b (h c p) d -> (b h) p c d", c=TILES, p=P)

    with ExitStack() as ctx:
        def sb(name, shape, dt=F32):
            return ctx.enter_context(nc.sbuf_tensor(name, shape, dt))

        def sem(name):
            return ctx.enter_context(nc.semaphore(name))

        def bank(name):
            return ctx.enter_context(nc.psum_tensor(name, [P, UNIT], F32))

        ident = sb("ident", [P, P])
        w1_f = sb("w1_f", [P, E, P])
        w1_hi = sb("w1_hi", [P, E, P], F32R)
        w1_lo = sb("w1_lo", [P, E, P], F32R)
        w2_f = sb("w2_f", [P, E, P])
        gate_f = sb("gate_f", [P, E])
        gate_hi = sb("gate_hi", [P, P], F32R)
        gate_lo = sb("gate_lo", [P, P], F32R)
        gate_bias = sb("gate_bias", [E, 1])
        att_w = sb("att_w", [P, 4, P])
        att_wT = sb("att_wT", [P, 4, P])
        NV = 6 + E
        rows = sb("rows", [NV, P])
        cols = sb("cols", [P, NV])
        neg_b1 = sb("neg_b1", [P, E])
        u_minus_w = sb("u_minus_w", [P, 1])
        w_minus_u = sb("w_minus_u", [P, 1])
        neg_2w = sb("neg_2w", [P, 1])
        b1_diag = sb("b1_diag", [P, E, 3 * E])
        b2_f = sb("b2_f", [3 * E, P])
        b2_all = sb("b2_all", [3 * E, P])
        b2_hi = sb("b2_hi", [3 * E, P], F32R)
        b2_lo = sb("b2_lo", [3 * E, P])
        table_in = sb("table_in", [P, 1])
        table_out = sb("table_out", [P, 1])
        low_row = sb("low_row", [3 * E, 2])
        b2_mix = sb("b2_mix", [3 * E, P])
        b2_stack = sb("b2_stack", [3 * E, P], F32R)
        prio = sb("prio", [P, 2 * TILES, E])
        col = {name: cols[:, k:k + 1] for k, name in enumerate(["tmk", "tmv", "tmr", "u", "w", "bo"])}

        XL = sb("XL", [P, 2, TILES, P])
        X0 = sb("X0", [P, 2, TILES, P])
        X1 = sb("X1", [P, 2, TILES, P])
        X2 = sb("X2", [P, 2, TILES, P])
        OUT = sb("OUT", [P, 2, TILES, P])
        LN = ["ffn0", "ln", "ffn1"]
        st = {k: sb(f"st_{k}", [P, TILES, 6]) for k in LN}
        mv = sb("mv", [P, 3, TILES, 2])
        var_eps = sb("var_eps", [P, 3, TILES])
        rstd = sb("rstd", [P, 3, TILES])
        newton = sb("newton", [P, 3, TILES])
        shift = sb("shift", [P, 3, TILES])
        Y = {k: sb(f"Y_{k}", [P, TILES, P]) for k in LN}
        y_hi = [sb(f"y_hi{f}", [P, 2, UNIT], F32R) for f in range(2)]
        y_lo = [sb(f"y_lo{f}", [P, 2, UNIT], F32R) for f in range(2)]
        y_all = [sb(f"y_all{f}", [P, UNIT]) for f in range(2)]
        scT = sb("scT", [E, 2, UNIT])
        sc = sb("sc", [P, 2 * TILES, E])
        top = sb("top", [P, 2 * TILES])
        hit = sb("hit", [P, 2 * TILES, E])
        sel1 = sb("sel1", [P, 2 * TILES, E])
        rest = sb("rest", [P, 2 * TILES, E])
        sel2 = sb("sel2", [P, 2 * TILES, E])
        both = sb("both", [P, 2 * TILES, E])
        comb = sb("comb", [P, 2 * TILES, 3 * E])
        comb_hi = sb("comb_hi", [P, 2 * TILES, E], F32R)
        combT = [sb(f"combT{f}", [E, 2, UNIT]) for f in range(2)]
        comb_stack = [sb(f"comb_stack{f}", [3 * E, 2, UNIT], F32R) for f in range(2)]
        comb_row = sb("comb_row", [P, E * UNIT])
        BC = sb("BC", [P, BC_RING, UNIT])
        G = sb("G", [P, G_RING, UNIT])
        ffn_oT = [sb(f"ffn_oT{f}", [P, UNIT]) for f in range(2)]
        yT = sb("yT", [P, 1 + T])
        diff = sb("diff", [P, UNIT])
        key_in = sb("key_in", [P, UNIT])
        val_in = sb("val_in", [P, UNIT])
        rec_in = sb("rec_in", [P, UNIT])
        rec_t = sb("rec_t", [P, UNIT])
        rec_s = sb("rec_s", [P, UNIT])
        over = sb("over", [P, UNIT])
        under = sb("under", [P, UNIT])
        e1 = sb("e1", [P, UNIT])
        e2 = sb("e2", [P, UNIT])
        ev = sb("ev", [P, UNIT])
        A_ = sb("A_", [P, T])
        B_ = sb("B_", [P, T])
        rcp = sb("rcp", [P, UNIT])
        wkv = sb("wkv", [P, UNIT])
        wkvr = sb("wkvr", [P, UNIT])
        att_oT = sb("att_oT", [P, UNIT])

        Z = [bank(f"Z{k}") for k in range(Z_BANKS)]
        ACC = bank("ACC")
        TR = bank("TR")
        SM = bank("SM")
        KR = bank("KR")
        VO = bank("VO")

        s_w1 = sem("w1_in")
        s_w2 = sem("w2_in")
        s_small = sem("vectors_in")
        s_b1in = sem("b1_in")
        s_b2in = sem("b2_in")
        s_attw = sem("attw_in")
        s_gate = sem("gate_in")
        s_zero = sem("zeroed")
        s_ident = sem("ident_made")
        s_prio = sem("prio_made")
        s_rowsT = sem("rows_turned")
        s_cols = sem("cols_made")
        s_vec = sem("vectors_made")
        s_w1hi = sem("w1_hi_made")
        s_w1lo = sem("w1_lo_made")
        s_ghi = sem("gate_hi_made")
        s_glo = sem("gate_lo_made")
        s_wT = sem("att_w_turned")
        s_wTs = sem("att_wT_made")
        s_b2m = sem("b1_w2_made")
        s_b2 = sem("b2_steps")
        x_in = [sem(f"x_in{q}") for q in range(2)]
        xl_in = [sem(f"xl_in{q}") for q in range(2)]
        stats = {k: sem(f"stats_{k}") for k in LN}
        moments = {k: sem(f"moments_{k}") for k in LN}
        rstd_step = sem("rstd_step")
        normed = {k: sem(f"normed_{k}") for k in LN}
        tr_full = sem("tr_full")
        sm_full = sem("sm_full")
        sc_copied = sem("sc_copied")
        all_made = [sem(f"all_made{f}") for f in range(2)]
        hi_made = [sem(f"hi_made{f}") for f in range(2)]
        lo_made = [sem(f"lo_made{f}") for f in range(2)]
        scT_made = [sem(f"scT_made{f}") for f in range(2)]
        gate_step = sem("gate_step")
        combT_made = [sem(f"combT_made{f}") for f in range(2)]
        row_in = [[sem(f"row_in{f}{q}") for q in range(2)] for f in range(2)]
        bc_made = sem("bc_made")
        z_full = sem("z_full")
        g_made = sem("g_made")
        g_used = sem("g_used")
        acc_read = sem("acc_read")
        x1_made = sem("x1_made")
        x2_made = sem("x2_made")
        out_made = sem("out_made")
        out_done = [sem(f"out_done{q}") for q in range(2)]
        yT_made = sem("yT_made")
        diff_made = sem("diff_made")
        mixed = sem("mixed")
        tanh_made = sem("tanh_made")
        rec_made = sem("rec_made")
        k_full = sem("k_full")
        v_full = sem("v_full")
        r_full = sem("r_full")
        o_full = sem("o_full")
        over_made = sem("over_made")
        under_made = sem("under_made")
        e1_made = sem("e1_made")
        e2_made = sem("e2_made")
        ev_made = sem("ev_made")
        a_made = sem("a_made")
        b_made = sem("b_made")
        rcp_made = sem("rcp_made")
        wkv_made = sem("wkv_made")
        wkvr_made = sem("wkvr_made")
        o_read = sem("o_read")

        read_by = {"res1_T": out_made, "ffn0_yT": all_made[0], "res0_T": x1_made, "oT": x2_made, "y2T": yT_made,
                   "ffn1_yT": all_made[1], "ffn0_score": scT_made[0], "ffn1_score": scT_made[1],
                   "scoreT": sc_copied,
                   "ffn0_combT": combT_made[0], "ffn1_combT": combT_made[1]}

        def apart(eng):
            eng.sem_inc(waited, 1)

        waited = sem("waited")
        block = ctx.enter_context(nc.Block())

        def walk(steps, s, on_block):
            here = [n for n, (f, unit, e) in enumerate(BLOCKS) if unit + 2 * f == s]
            blocks = iter(here)
            for item in order(s):
                if item == "F":
                    n = next(blocks, None)
                    if n is not None:
                        on_block(n)
                    continue
                step, off = item
                if step in steps and present(step, off, s):
                    steps[step](s, s + off if off is not None else None)

        def pipeline(eng, before, one_slot):
            before()
            for s in range(FIRST_SLOT, 2 * HEAD_TURNS):
                one_slot(Turn(), s)
            with eng.Fori(HEAD_TURNS, UNITS // 2 - TAIL_TURNS) as it:
                for s in (2 * WRITTEN, 2 * WRITTEN + 1):
                    one_slot(Turn(it), s)
            for s in range(UNITS - 2 * TAIL_TURNS, SLOTS):
                one_slot(Turn(), s)

        @block.sync
        def _(sp):
            def load(t, unit, dst, done):
                src = x_u[t.v(unit, 2)] if t.it is not None else x_u[unit]
                sp.dma_start(dst[:, unit % 2], src).then_inc(done[unit % 2], 16)

            def one_slot(t, s):
                def ffn_row(f):
                    def step(s, unit):
                        q = unit % 2
                        sp.wait_ge(combT_made[f], t.v(unit + 1, 2))
                        apart(sp)
                        if unit >= 2:
                            sp.wait_ge(bc_made, t.v(FIRST[f, unit - 2] + E, PER))
                        at = 32 * (2 * f + q)
                        sp.dma_start(comb_row[at:at + 1].rearrange("p (e n) -> p e n", e=E),
                                     combT[f][:, q]).then_inc(row_in[f][q], 16)
                    return step

                def load_sum(s, unit):
                    if exists(unit + 2):
                        sp.wait_ge(x1_made, t.v(unit + 1, 2))
                        load(t, unit + 2, X0, x_in)

                def load_ln(s, unit):
                    if exists(unit + 2):
                        sp.wait_ge(normed["ffn0"], t.v(unit + 1, 2))
                        load(t, unit + 2, XL, xl_in)

                def store(s, unit):
                    q = unit % 2
                    sp.wait_ge(out_made, t.v(unit + 1, 2))
                    dst = out_u[t.v(unit, 2)] if t.it is not None else out_u[unit]
                    sp.dma_start(dst, OUT[:, q]).then_inc(out_done[q], 16)

                walk({"res0": load_sum, "ffn0_lo": load_ln, "res1": store, "ffn0_combT": ffn_row(0), "ffn1_combT": ffn_row(1)},
                     s, lambda n: None)

            def before():
                for q in range(2):
                    sp.sem_inc(out_done[q], 16)
                load(Turn(), 0, XL, xl_in)
                sp.dma_start(gate_f[:], gate_w).then_inc(s_gate, 16)
                sp.dma_start(gate_bias[:], gate_b.rearrange("(e a) -> e a", a=1)).then_inc(s_gate, 16)
                load(Turn(), 1, XL, xl_in)
                sp.dma_start(att_w[:, 0], wk).then_inc(s_attw, 16)
                sp.dma_start(att_w[:, 1], wv).then_inc(s_attw, 16)
                sp.dma_start(att_w[:, 2], wr).then_inc(s_attw, 16)
                sp.dma_start(att_w[:, 3], wo).then_inc(s_attw, 16)
                load(Turn(), 0, X0, x_in)
                load(Turn(), 1, X0, x_in)

            pipeline(sp, before, one_slot)
            for q in range(2):
                sp.wait_ge(out_done[q], 16 + 16 * UNITS // 2)

        @block.gpsimd
        def _(pool):
            def before():
                nc.gpsimd.memset(table_in[:], 0.0)
                nc.gpsimd.memset(ident[:], 0.0).then_inc(s_zero, 1)
                pool.wait_ge(s_zero, 1)
                nc.gpsimd.affine_select(out=ident[:], in_=ident[:], compare_op=ALU.not_equal, fill=1.0, base=0,
                                        pattern=[[-1, P]], channel_multiplier=1).then_inc(s_ident, 1)
                for k, v in enumerate([tmk, tmv, tmr, u, w, bo]):
                    pool.dma_start(rows[k:k + 1, :], v.rearrange("(a d) -> a d", a=1)).then_inc(s_small, 16)

            def broadcast(t, n):
                f, unit, e = BLOCKS[n]
                if e == 0:
                    pool.wait_ge(row_in[f][unit % 2], t.v(16 * (unit // 2 + 1), 16))
                if n >= BC_RING:
                    pool.wait_ge(g_made, t.v(n - BC_RING + 1, PER))
                apart(pool)
                at = 32 * (2 * f + unit % 2)
                nc.gpsimd.partition_broadcast(
                    BC[:, n % BC_RING], comb_row[at:at + 1, e * UNIT:(e + 1) * UNIT]).then_inc(bc_made, 1)

            def one_slot(t, s):
                def head(f):
                    def step(s, unit):
                        for e in range(BC_AHEAD):
                            broadcast(t, FIRST[f, unit] + e)
                    return step

                def on_block(n):
                    if BLOCKS[n][2] + BC_AHEAD < E:
                        broadcast(t, n + BC_AHEAD)

                walk({"ffn0_head": head(0), "ffn1_head": head(1)}, s, on_block)

            pipeline(pool, before, one_slot)

        @block.scalar
        def _(act):
            def before():
                act.dma_start(w1_f[:], w1.rearrange("e d h -> d e h")).then_inc(s_w1, 16)
                act.dma_start(rows[6:6 + E, :], b1).then_inc(s_b1in, 16)
                act.dma_start(w2_f[:], w2.rearrange("e h d -> h e d")).then_inc(s_w2, 16)
                for k in range(3):
                    act.dma_start(b2_f[k * E:(k + 1) * E, :], b2).then_inc(s_b2in, 16)
                act.wait_ge(s_zero, 1)
                nc.scalar.activation(table_out[:], table_in[:], ACT.Exp)

            def one_slot(t, s):
                def norm(k, X):
                    at = LN.index(k)

                    def step(s, unit):
                        made_in = unit - SHARED["rstd0"][at]
                        act.wait_ge(rstd_step, t.v(RSTD_STEPS * (made_in - FIRST_SLOT + 1), 2 * RSTD_STEPS))
                        if unit >= 1:
                            yT_step = {"ffn0": "ffn0_yT", "ln": "y2T", "ffn1": "ffn1_yT"}[k]
                            act.wait_ge(tr_full, t.v(uses(yT_step, unit - 1 - OFF[yT_step]) + 1, TR_PER))
                        for c in range(TILES):
                            last = nc.scalar.activation(Y[k][:, c], X[:, unit % 2, c], ACT.Identity,
                                                        bias=shift[:, at, c:c + 1], scale=rstd[:, at, c:c + 1])
                        last.then_inc(normed[k], 1)
                    return step

                def y_high(f):
                    def step(s, unit):
                        act.wait_ge(tr_full, t.v(uses(f"ffn{f}_yT", s) + 1, TR_PER))
                        if unit >= 2:
                            act.wait_ge(z_full, t.v(FIRST[f, unit - 2] + E, PER))
                            act.wait_ge(sm_full, t.v(uses(f"ffn{f}_score", unit - 2 - OFF[f"ffn{f}_score"]) + 1, SM_PER))
                        if unit >= 1:
                            act.wait_ge(lo_made[f], t.v(unit, 2))
                        nc.scalar.activation(y_all[f][:], TR[:], ACT.Copy).then_inc(all_made[f], 1)
                        act.wait_ge(all_made[f], t.v(unit + 1, 2))
                        nc.scalar.activation(y_hi[f][:, unit % 2], y_all[f][:], ACT.Copy).then_inc(hi_made[f], 1)
                    return step

                def score(f):
                    def step(s, unit):
                        n = uses(f"ffn{f}_score", s)
                        if unit == 0 and f == 0:
                            act.wait_ge(s_gate, 32)
                        act.wait_ge(sm_full, t.v(n + 1, SM_PER))
                        nc.scalar.activation(scT[:, f], SM[0:E], ACT.Identity, bias=gate_bias[:, 0:1]).then_inc(scT_made[f], 1)
                    return step

                def comb_turned(f):
                    def step(s, unit):
                        act.wait_ge(sm_full, t.v(uses(f"ffn{f}_combT", s) + 1, SM_PER))
                        if unit >= 2:
                            act.wait_ge(row_in[f][unit % 2], t.v(16 * (unit // 2), 16))
                            act.wait_ge(g_used, t.v(FIRST[f, unit - 2] + 1, PER))
                        nc.scalar.activation(comb_stack[f][:, unit % 2], SM[0:3 * E], ACT.Copy)
                        nc.scalar.activation(combT[f][:, unit % 2], SM[0:E], ACT.Copy).then_inc(combT_made[f], 1)
                    return step

                def y2_turned(s, unit):
                    lo = (unit % 2) * UNIT
                    act.wait_ge(tr_full, t.v(uses("y2T", s) + 1, TR_PER))
                    if unit >= 1:
                        act.wait_ge(mixed, t.v(3 * unit, 6))
                    nc.scalar.activation(yT[:, lo + 1:lo + 1 + UNIT], TR[:], ACT.Copy).then_inc(yT_made, 1)

                def receptance(s, unit):
                    act.wait_ge(mixed, t.v(3 * unit + 1, 6))
                    if unit >= 1:
                        act.wait_ge(r_full, t.v(unit, 2))
                    nc.scalar.activation(rec_t[:], rec_in[:], ACT.Tanh, scale=0.5).then_inc(tanh_made, 1)
                    act.wait_ge(tanh_made, t.v(unit + 1, 2))
                    nc.scalar.activation(rec_s[:], rec_t[:], ACT.Copy, bias=0.5, scale=0.5).then_inc(rec_made, 1)

                def decays(s, unit):
                    if unit == 0:
                        act.wait_ge(s_vec, 4)
                    act.wait_ge(k_full, t.v(unit + 1, 2))
                    nc.scalar.activation(over[:], KR[:], ACT.Relu, bias=u_minus_w[:, 0:1]).then_inc(over_made, 1)
                    nc.scalar.activation(under[:], KR[:], ACT.Relu, bias=w_minus_u[:, 0:1], scale=-1.0).then_inc(under_made, 1)
                    act.wait_ge(over_made, t.v(unit + 1, 2))
                    if unit >= 1:
                        act.wait_ge(b_made, t.v(unit, 2))
                    nc.scalar.activation(e1[:], over[:], ACT.Exp, bias=neg_2w[:, 0:1], scale=-1.0).then_inc(e1_made, 1)
                    act.wait_ge(under_made, t.v(unit + 1, 2))
                    nc.scalar.activation(e2[:], under[:], ACT.Exp, scale=-1.0).then_inc(e2_made, 1)

                def att_out(s, unit):
                    act.wait_ge(o_full, t.v(unit + 1, 2))
                    if unit >= 1:
                        act.wait_ge(tr_full, t.v(uses("oT", unit - 1 - OFF["oT"]) + 1, TR_PER))
                    nc.scalar.activation(att_oT[:], VO[:], ACT.Identity, bias=col["bo"]).then_inc(o_read, 1)

                def on_block(n):
                    f, unit, e = BLOCKS[n]
                    if e != E - 1:
                        return
                    act.wait_ge(g_used, t.v(n + 1, PER))
                    if unit >= 1:
                        act.wait_ge(tr_full, t.v(uses(f"res{f}_T", unit - 1 - OFF[f"res{f}_T"]) + 1, TR_PER))
                    nc.scalar.activation(ffn_oT[f][:], ACC[:], ACT.Copy, scale=0.5).then_inc(acc_read, 1)

                walk({"ffn0_norm": norm("ffn0", XL), "ln_norm": norm("ln", X1), "ffn1_norm": norm("ffn1", X2),
                      "ffn0_yT": y_high(0), "ffn1_yT": y_high(1), "ffn0_score": score(0), "ffn1_score": score(1),
                      "ffn0_combT": comb_turned(0), "ffn1_combT": comb_turned(1), "y2T": y2_turned,
                      "sigmoid": receptance, "kv": decays, "o": att_out}, s, on_block)

            pipeline(act, before, one_slot)

        @block.vector
        def _(dve):
            def before():
                nc.vector.memset(yT[:, 0:1], 0.0)
                nc.vector.memset(b1_diag[:], 0.0)
                nc.vector.memset(mv[:], 1.0)
                nc.vector.memset(sc[:], 0.0)
                for e in range(E):
                    nc.vector.memset(prio[:, :, e:e + 1], float(E - e))
                nc.vector.memset(gate_hi[:].bitcast(F32), 0.0)
                nc.vector.memset(gate_lo[:].bitcast(F32), 0.0).then_inc(s_prio, 1)
                dve.wait_ge(s_prio, 1)

            def split_gate_w(s, unit):
                dve.wait_ge(s_gate, 32)
                nc.vector.tensor_copy(gate_hi[:, 0:E], gate_f[:]).then_inc(s_ghi, 1)
                dve.wait_ge(s_ghi, 1)
                nc.vector.tensor_tensor(gate_lo[:, 0:E], gate_f[:], gate_hi[:, 0:E].bitcast(F32),
                                        ALU.subtract).then_inc(s_glo, 1)

            def split_w1(s, unit):
                dve.wait_ge(s_w1, 16)
                nc.vector.tensor_copy(w1_hi[:], w1_f[:]).then_inc(s_w1hi, 1)
                dve.wait_ge(s_w1hi, 1)
                nc.vector.tensor_tensor(w1_lo[:], w1_f[:], w1_hi[:].bitcast(F32), ALU.subtract).then_inc(s_w1lo, 1)

            def vectors(s, unit):
                dve.wait_ge(s_rowsT, 1)
                nc.vector.tensor_copy(cols[:], KR[:, 0:NV]).then_inc(s_cols, 1)
                dve.wait_ge(s_cols, 1)
                nc.vector.tensor_scalar(neg_b1[:], cols[:, 6:NV], -1.0, None, ALU.mult).then_inc(s_vec, 1)
                nc.vector.tensor_tensor(u_minus_w[:], col["u"], col["w"], ALU.subtract).then_inc(s_vec, 1)
                nc.vector.tensor_tensor(w_minus_u[:], col["w"], col["u"], ALU.subtract).then_inc(s_vec, 1)
                nc.vector.tensor_scalar(neg_2w[:], col["w"], -2.0, None, ALU.mult).then_inc(s_vec, 1)
                diagonal = b1_diag[:].rearrange("p e n -> p (e n)")
                for k in range(3):
                    last = nc.vector.tensor_copy(diagonal[:, k * E::3 * E + 1], cols[:, 6:NV])
                last.then_inc(s_cols, 1)

            def stack_b2(s, unit):
                dve.wait_ge(s_b2m, 1)
                dve.wait_ge(s_b2in, 48)
                nc.vector.tensor_tensor(b2_all[:], VO[0:3 * E, 0:P], b2_f[:], ALU.add).then_inc(s_b2, 1)
                nc.vector.tensor_reduce(low_row[:, 0:1], ident[0:3 * E, 2 * E:3 * E], AX.X, ALU.add).then_inc(s_b2, 1)
                dve.wait_ge(s_b2, 2)
                nc.vector.tensor_copy(b2_hi[:], b2_all[:]).then_inc(s_b2, 1)
                nc.vector.tensor_scalar(low_row[:, 1:2], low_row[:, 0:1], -1.0, 1.0, ALU.mult, ALU.add).then_inc(s_b2, 1)
                dve.wait_ge(s_b2, 4)
                nc.vector.tensor_tensor(b2_lo[:], b2_all[:], b2_hi[:].bitcast(F32), ALU.subtract).then_inc(s_b2, 1)
                nc.vector.tensor_scalar(b2_mix[:], b2_hi[:].bitcast(F32), low_row[:, 1:2], None, ALU.mult).then_inc(s_b2, 1)
                dve.wait_ge(s_b2, 6)
                nc.vector.scalar_tensor_tensor(out=b2_stack[:], in0=b2_lo[:], scalar=low_row[:, 0:1], in1=b2_mix[:],
                                               op0=ALU.mult, op1=ALU.add).then_inc(s_b2, 1)

            def copy_att_w(s, unit):
                dve.wait_ge(s_wT, 1)
                nc.vector.tensor_copy(att_wT[:].rearrange("p a b -> p (a b)"), KR[:]).then_inc(s_wTs, 1)

            def one_slot(t, s):
                def stat(k, X):
                    at = LN.index(k)

                    def step(s, unit):
                        if k == "ffn0":
                            dve.wait_ge(xl_in[unit % 2], t.v(16 * (unit // 2 + 1), 16))
                        else:
                            dve.wait_ge({"ln": x1_made, "ffn1": x2_made}[k], t.v(unit + 1, 2))
                        for c in range(TILES):
                            last = nc.vector.bn_stats(st[k][:, c], X[:, unit % 2, c])
                        last.then_inc(stats[k], 1)
                        dve.wait_ge(stats[k], t.v(unit + 1, 2))
                        apart(dve)
                        for c in range(TILES):
                            last = nc.vector.bn_aggr(mv[:, at, c], st[k][:, c])
                        last.then_inc(moments[k], 1)
                    return step

                def rstd_part(k):
                    def step(s, unit):
                        if k == 0:
                            for name, off in zip(LN, SHARED["rstd0"]):
                                if exists(s + off):
                                    dve.wait_ge(moments[name], t.v(s + off + 1, 2))
                                if exists(s - 1 + off):
                                    dve.wait_ge(normed[name], t.v(s + off, 2))
                            last = nc.vector.tensor_scalar(var_eps[:], mv[:, :, :, 1], LN_EPS, None, ALU.add)
                        else:
                            dve.wait_ge(rstd_step, t.v(RSTD_STEPS * (s - FIRST_SLOT) + k, 2 * RSTD_STEPS))
                        if k == 1:
                            last = nc.vector.tensor_scalar(rstd[:].bitcast(I32), var_eps[:].bitcast(I32), -0.5,
                                                           RSQRT_MAGIC, ALU.mult, ALU.add)
                        elif k == RSTD_STEPS - 1:
                            last = nc.vector.scalar_tensor_tensor(out=shift[:], in0=mv[:, :, :, 0], scalar=-1.0,
                                                                  in1=rstd[:], op0=ALU.mult, op1=ALU.mult)
                        elif k > 1 and k % 3 == 2:
                            last = nc.vector.tensor_tensor(newton[:], rstd[:], rstd[:], ALU.mult)
                        elif k > 1 and k % 3 == 0:
                            last = nc.vector.scalar_tensor_tensor(out=newton[:], in0=newton[:], scalar=-0.5,
                                                                  in1=var_eps[:], op0=ALU.mult, op1=ALU.mult)
                        elif k > 1:
                            last = nc.vector.scalar_tensor_tensor(out=rstd[:], in0=newton[:], scalar=1.5,
                                                                  in1=rstd[:], op0=ALU.add, op1=ALU.mult)
                        last.then_inc(rstd_step, 1)
                    return step

                def y_low(f):
                    def step(s, unit):
                        dve.wait_ge(hi_made[f], t.v(unit + 1, 2))
                        nc.vector.tensor_tensor(y_lo[f][:, unit % 2], y_all[f][:], y_hi[f][:, unit % 2].bitcast(F32),
                                                ALU.subtract).then_inc(lo_made[f], 1)
                    return step

                def wide(a):
                    return a[:].unsqueeze(2).to_broadcast([P, 2 * TILES, E])

                def gate_part(k):
                    def step(s, unit):
                        V, TT = nc.vector, nc.vector.tensor_tensor
                        has = [exists(s + off) for off in SHARED["gate0"]]
                        lo, hi = (0 if has[0] else TILES), (2 * TILES if has[1] else TILES)
                        if k == 0:
                            dve.wait_ge(sm_full, t.v(uses("scoreT", s) + 1, SM_PER))
                            V.tensor_copy(sc[:, lo:hi].rearrange("p c e -> p (c e)"),
                                          SM[:, lo * E:hi * E]).then_inc(sc_copied, 1)
                            return
                        if k == 1:
                            dve.wait_ge(sc_copied, t.v(s + 2, 2))
                        else:
                            done = k - 1 if k < GATE_PARTS - 1 else GATE_STEPS - 1
                            dve.wait_ge(gate_step, t.v(GATE_STEPS * (s + 1) + done, 2 * GATE_STEPS))
                        if k == 1 or k == 7:
                            last = V.tensor_reduce(top[:], (sc if k == 1 else rest)[:], AX.X, ALU.max)
                        elif k == 2 or k == 8:
                            last = TT(hit[:], (sc if k == 2 else rest)[:], wide(top), ALU.is_equal)
                        elif k == 3 or k == 9:
                            last = TT(hit[:], hit[:], prio[:], ALU.mult)
                        elif k == 4 or k == 10:
                            last = V.tensor_reduce(top[:], hit[:], AX.X, ALU.max)
                        elif k == 5 or k == 11:
                            last = TT((sel1 if k == 5 else sel2)[:], hit[:], wide(top), ALU.is_equal)
                        elif k == 6:
                            last = V.scalar_tensor_tensor(out=rest[:], in0=sel1[:], scalar=-3.0e38, in1=sc[:],
                                                          op0=ALU.mult, op1=ALU.add)
                        elif k == 12:
                            last = TT(both[:], sel1[:], sel2[:], ALU.add)
                        elif k == 13:
                            TT(comb[:, :, 0:E], both[:], sc[:], ALU.mult).then_inc(gate_step, 1)
                            TT(comb[:, :, 2 * E:3 * E], both[:], sc[:], ALU.mult)
                            last = TT(comb_hi[:], both[:], sc[:], ALU.mult)
                        elif k == 14:
                            last = TT(comb[:, :, E:2 * E], comb[:, :, 0:E], comb_hi[:].bitcast(F32), ALU.subtract)
                        last.then_inc(gate_step, 1)
                    return step

                def residual(name, src, dst, made):
                    def step(s, unit):
                        q = unit % 2
                        n = uses(name, s)
                        dve.wait_ge(tr_full, t.v(n + 1, TR_PER))
                        if name == "res0_T":
                            dve.wait_ge(x_in[q], t.v(16 * (unit // 2 + 1), 16))
                        if name == "res1_T" and unit >= 2:
                            dve.wait_ge(out_done[q], t.v(16 + 16 * (unit // 2), 16))
                        nc.vector.tensor_tensor(dst[:, q].rearrange("p c d -> p (c d)"),
                                                src[:, q].rearrange("p c d -> p (c d)"), TR[:], ALU.add).then_inc(made, 1)
                    return step

                def mix(s, unit):
                    lo = (unit % 2) * UNIT
                    dve.wait_ge(yT_made, t.v(unit + 1, 2))
                    nc.vector.tensor_tensor(diff[:], yT[:, lo + 1:lo + 1 + UNIT], yT[:, lo:lo + UNIT],
                                            ALU.subtract).then_inc(diff_made, 1)
                    dve.wait_ge(diff_made, t.v(unit + 1, 2))
                    if unit >= 1:
                        dve.wait_ge(v_full, t.v(unit, 2))
                        dve.wait_ge(tanh_made, t.v(unit, 2))
                    for name, dst in (("tmr", rec_in), ("tmk", key_in), ("tmv", val_in)):
                        nc.vector.scalar_tensor_tensor(out=dst[:], in0=diff[:], scalar=col[name], in1=yT[:, lo:lo + UNIT],
                                                       op0=ALU.mult, op1=ALU.add).then_inc(mixed, 1)

                def scans(s, unit):
                    lo = (unit % 2) * UNIT
                    dve.wait_ge(e2_made, t.v(unit + 1, 2))
                    dve.wait_ge(v_full, t.v(unit + 1, 2))
                    nc.vector.tensor_tensor(ev[:], VO[:], e2[:], ALU.mult).then_inc(ev_made, 1)
                    first = unit % 2 == 0
                    if not first:
                        dve.wait_ge(b_made, t.v(unit, 2))
                    nc.vector.tensor_tensor_scan(B_[:, lo:lo + UNIT], e1[:], e2[:], 0.0 if first else B_[:, lo - 1:lo],
                                                 ALU.mult, ALU.add).then_inc(b_made, 1)
                    dve.wait_ge(ev_made, t.v(unit + 1, 2))
                    nc.vector.tensor_tensor_scan(A_[:, lo:lo + UNIT], e1[:], ev[:], 0.0 if first else A_[:, lo - 1:lo],
                                                 ALU.mult, ALU.add).then_inc(a_made, 1)

                def rcp_part(k):
                    def step(s, unit):
                        lo = (unit % 2) * UNIT
                        if k == 0:
                            dve.wait_ge(b_made, t.v(unit + 1, 2))
                        nc.vector.reciprocal(rcp[:, k * P:(k + 1) * P], B_[:, lo + k * P:lo + (k + 1) * P]).then_inc(rcp_made, 1)
                    return step

                def weigh(s, unit):
                    lo = (unit % 2) * UNIT
                    dve.wait_ge(rcp_made, t.v(TILES * (unit + 1), 2 * TILES))
                    dve.wait_ge(a_made, t.v(unit + 1, 2))
                    nc.vector.tensor_tensor(wkv[:], A_[:, lo:lo + UNIT], rcp[:], ALU.mult).then_inc(wkv_made, 1)
                    dve.wait_ge(wkv_made, t.v(unit + 1, 2))
                    dve.wait_ge(r_full, t.v(unit + 1, 2))
                    if unit >= 1:
                        dve.wait_ge(o_full, t.v(unit, 2))
                    nc.vector.tensor_tensor(wkvr[:], KR[:], wkv[:], ALU.mult).then_inc(wkvr_made, 1)

                def on_block(n):
                    f, unit, e = BLOCKS[n]
                    dve.wait_ge(z_full, t.v(n + 1, PER))
                    dve.wait_ge(bc_made, t.v(n + 1, PER))
                    if n >= G_RING:
                        dve.wait_ge(g_used, t.v(n - G_RING + 1, PER))
                    nc.vector.scalar_tensor_tensor(out=G[:, n % G_RING], in0=Z[z_bank(n)][:], scalar=neg_b1[:, e:e + 1],
                                                   in1=BC[:, n % BC_RING], op0=ALU.max, op1=ALU.mult).then_inc(g_made, 1)

                steps = {"ffn0_stat": stat("ffn0", XL), "ln_stat": stat("ln", X1), "ffn1_stat": stat("ffn1", X2),
                         "ffn0_lo": y_low(0), "ffn1_lo": y_low(1), 
                         "res0": residual("res0_T", X0, X1, x1_made), "x2": residual("oT", X1, X2, x2_made),
                         "res1": residual("res1_T", X2, OUT, out_made), "mix": mix, "ev": scans, "wkv": weigh}
                steps |= {f"rcp{k}": rcp_part(k) for k in range(TILES)}
                steps |= {f"rstd{k}": rstd_part(k) for k in range(RSTD_STEPS)}
                steps |= {f"gate{k}": gate_part(k) for k in range(GATE_PARTS)}
                steps |= {"gate_w": split_gate_w, "w1": split_w1, "vectors": vectors, "b2": stack_b2, "att_w": copy_att_w}
                walk(steps, s, on_block)

            pipeline(dve, before, one_slot)

        @block.tensor
        def _(pe):
            def before():
                pe.wait_ge(s_ident, 1)

            def turn_rows(s, unit):
                pe.wait_ge(s_small, 16 * 6)
                pe.wait_ge(s_b1in, 16)
                nc.tensor.transpose(KR[:, 0:NV], rows[:], ident[0:NV, 0:NV]).then_inc(s_rowsT, 1)

            def b1_w2(s, unit):
                pe.wait_ge(s_w2, 16)
                pe.wait_ge(s_cols, 2)
                for e in range(E):
                    last = nc.tensor.matmul(VO[0:3 * E, 0:P], b1_diag[:, e], w2_f[:, e], start=(e == 0), stop=(e == E - 1))
                last.then_inc(s_b2m, 1)

            def turn_att_w(s, unit):
                pe.wait_ge(s_cols, 1)
                pe.wait_ge(s_attw, 64)
                for k in range(4):
                    last = nc.tensor.transpose(KR[:, k * P:(k + 1) * P], att_w[:, k], ident[:])
                last.then_inc(s_wT, 1)

            def first_z(s, unit):
                pe.wait_ge(s_w1lo, 1)
                for n in range(Z_AHEAD):
                    up(Turn(), n)

            def up(t, n):
                f, unit, e = BLOCKS[n]
                if e == 0:
                    pe.wait_ge(lo_made[f], t.v(unit + 1, 2))
                if (k := z_before(n)) is not None:
                    pe.wait_ge(g_made, t.v(k + 1, PER))
                z = Z[z_bank(n)][:]
                q = unit % 2
                nc.tensor.matmul(z, w1_hi[:, e], y_hi[f][:, q], start=True, stop=False)
                nc.tensor.matmul(z, w1_hi[:, e], y_lo[f][:, q], start=False, stop=False)
                nc.tensor.matmul(z, w1_lo[:, e], y_hi[f][:, q], start=False, stop=True).then_inc(z_full, 1)

            def down(t, n):
                f, unit, e = BLOCKS[n]
                if e == 0:
                    if n >= E:
                        pe.wait_ge(acc_read, t.v(n // E, 4))
                    pe.wait_ge(combT_made[f], t.v(unit + 1, 2))
                    if n == 0:
                        pe.wait_ge(s_b2, 7)
                    nc.tensor.matmul(ACC[:], b2_stack[:], comb_stack[f][:, unit % 2], start=True, stop=False)
                pe.wait_ge(g_made, t.v(n + 1, PER))
                last = nc.tensor.matmul(ACC[:], w2_f[:, e], G[:, n % G_RING], start=False, stop=(e == E - 1))
                last.then_inc(g_used, 1)

            def one_slot(t, s):
                def bank_read(table, step, s):
                    if (past := last_use(table, step, s)) is not None:
                        pe.wait_ge(read_by[past[0]], t.v(past[1], 2))

                def turn(step_name, source, wait):
                    def step(s, unit):
                        bank_read(TR_USES, step_name, s)
                        wait(unit)
                        for c in range(TILES):
                            last = nc.tensor.transpose(TR[:, c * P:(c + 1) * P], source(c), ident[:])
                        last.then_inc(tr_full, 1)
                    return step

                def y_turn(name, k):
                    return turn(name, lambda c: Y[k][:, c], lambda unit: pe.wait_ge(normed[k], t.v(unit + 1, 2)))

                def ffn_turn(f):
                    return turn(f"res{f}_T", lambda c: ffn_oT[f][:, c * P:(c + 1) * P],
                                lambda unit: pe.wait_ge(acc_read, t.v(FIRST[f, unit] // E + 1, 4)))

                def score(f):
                    def step(s, unit):
                        bank_read(SM_USES, f"ffn{f}_score", s)
                        pe.wait_ge(lo_made[f], t.v(unit + 1, 2))
                        if unit == 0 and f == 0:
                            pe.wait_ge(s_glo, 1)
                        q = unit % 2
                        nc.tensor.matmul(SM[:], gate_hi[:], y_hi[f][:, q], start=True, stop=False)
                        nc.tensor.matmul(SM[:], gate_hi[:], y_lo[f][:, q], start=False, stop=False)
                        nc.tensor.matmul(SM[:], gate_lo[:], y_hi[f][:, q], start=False, stop=True).then_inc(sm_full, 1)
                    return step

                def scores_back(s, unit):
                    bank_read(SM_USES, "scoreT", s)
                    for f, off in enumerate(SHARED["scoreT"]):
                        if exists(s + off):
                            pe.wait_ge(scT_made[f], t.v(s + off + 1, 2))
                            apart(pe)
                            for c in range(TILES):
                                at = (f * TILES + c) * E
                                last = nc.tensor.transpose(SM[:, at:at + E], scT[:, f, c * P:(c + 1) * P], ident[0:E, 0:E])
                    last.then_inc(sm_full, 1)

                def comb_turn(f):
                    def step(s, unit):
                        bank_read(SM_USES, f"ffn{f}_combT", s)
                        pe.wait_ge(gate_step, t.v(GATE_STEPS * (s + 2), 2 * GATE_STEPS))
                        for c in range(TILES):
                            last = nc.tensor.transpose(SM[0:3 * E, c * P:(c + 1) * P], comb[:, f * TILES + c], ident[:])
                        last.then_inc(sm_full, 1)
                    return step

                def keys_values(s, unit):
                    if unit == 0:
                        pe.wait_ge(s_wTs, 1)
                    pe.wait_ge(mixed, t.v(3 * (unit + 1), 6))
                    if unit >= 1:
                        pe.wait_ge(wkvr_made, t.v(unit, 2))
                        pe.wait_ge(o_read, t.v(unit, 2))
                    nc.tensor.matmul(KR[:], att_wT[:, 0], key_in[:], start=True, stop=True).then_inc(k_full, 1)
                    nc.tensor.matmul(VO[:], att_wT[:, 1], val_in[:], start=True, stop=True).then_inc(v_full, 1)

                def receptance(s, unit):
                    pe.wait_ge(under_made, t.v(unit + 1, 2))
                    pe.wait_ge(rec_made, t.v(unit + 1, 2))
                    nc.tensor.matmul(KR[:], att_wT[:, 2], rec_s[:], start=True, stop=True).then_inc(r_full, 1)

                def output(s, unit):
                    pe.wait_ge(ev_made, t.v(unit + 1, 2))
                    pe.wait_ge(wkvr_made, t.v(unit + 1, 2))
                    nc.tensor.matmul(VO[:], att_wT[:, 3], wkvr[:], start=True, stop=True).then_inc(o_full, 1)

                def late(unit, f):
                    return unit + 2 * f >= UNITS

                def head(s, unit):
                    if late(unit, 1):
                        for e in range(Z_AHEAD):
                            up(t, FIRST[1, unit] + e)

                def on_block(n):
                    if n + Z_AHEAD < len(BLOCKS):
                        f, unit, e = BLOCKS[n + Z_AHEAD]
                        if not (late(unit, f) and e < Z_AHEAD):
                            up(t, n + Z_AHEAD)
                    down(t, n)

                walk({"res0_T": ffn_turn(0), "res1_T": ffn_turn(1), "ffn0_yT": y_turn("ffn0_yT", "ffn0"),
                      "y2T": y_turn("y2T", "ln"), "ffn1_yT": y_turn("ffn1_yT", "ffn1"),
                      "oT": turn("oT", lambda c: att_oT[:, c * P:(c + 1) * P], lambda unit: pe.wait_ge(o_read, t.v(unit + 1, 2))),
                      "ffn0_score": score(0), "ffn1_score": score(1), "scoreT": scores_back,
                      "ffn0_combT": comb_turn(0), "ffn1_combT": comb_turn(1),
                      "kv": keys_values, "r": receptance, "o": output, "ffn1_head": head,
                      "rows": turn_rows, "b2_rows": b1_w2, "att_turn": turn_att_w, "first_z": first_z}, s, on_block)

            pipeline(pe, before, one_slot)


_INS = ['L0_attn_x', 'L0_attn_u', 'L0_attn_w', 'L0_attn_tmk', 'L0_attn_tmv', 'L0_attn_tmr', 'L0_attn_Wk', 'L0_attn_Wv',
        'L0_attn_Wr', 'L0_attn_Wo', 'L0_attn_bo', 'L0_ffn_gate_w', 'L0_ffn_gate_b', 'L0_ffn_w1', 'L0_ffn_b1',
        'L0_ffn_w2', 'L0_ffn_b2']


def kernel(**inputs):
    import numpy as np
    import concourse.bacc as bacc
    from concourse.bass_utils import run_bass_kernel_spmd

    nc = bacc.Bacc("TRN2", target_bir_lowering=False, num_devices=1)
    arrays, args = {}, []
    for name in _INS:
        a = np.ascontiguousarray(inputs[name])
        arrays[f"in_{name}"] = a
        args.append(nc.dram_tensor(f"in_{name}", a.shape, mybir.dt.from_np(a.dtype), kind="ExternalInput").ap())
    shape = inputs["L0_attn_x"].shape
    out = nc.dram_tensor("out", shape, F32, kind="ExternalOutput").ap()
    macaron_kernel(nc, *args, out)
    r = run_bass_kernel_spmd(nc, [arrays], core_ids=[0])
    return r.results[0]["out"]
```
